# Optimizing a Trainium2 kernel written in Bass

```python
import numpy as np
import jax
import jax.numpy as jnp

def _softmax(x, axis=-1):
    return jax.nn.softmax(x, axis=axis)

def _gelu(x):
    return jax.nn.gelu(x, approximate=True)

def _silu(x):
    return jax.nn.silu(x)

def _sigmoid(x):
    return jax.nn.sigmoid(x)

def _layernorm(x, axis=-1, eps=1e-05):
    m = jnp.mean(x, axis=axis, keepdims=True)
    v = jnp.var(x, axis=axis, keepdims=True)
    return (x - m) / jnp.sqrt(v + eps)

def _scatter_add(tgt, idx, src, axis=0):
    return tgt.at[idx].add(src)

def _segment_sum(src, seg, n):
    return jax.ops.segment_sum(src, seg, n)
kernel_name = 'mk_xattn_ffn_d1_seqx_r2_e051df'

def setup_inputs(seed: int=0):
    np.random.seed(seed)
    _w = jnp.asarray

    def _rec_inputs():
        import jax
        import jax.numpy as jnp
        _rk = jax.random.key(seed)
        x = -0.0002928 + 1 * jax.random.normal(jax.random.fold_in(_rk, 1), (8, 512, 512), jnp.float32)
        _lenS = 512 - jax.random.randint(jax.random.fold_in(_rk, 7), (8,), 0, max(1, 512 // 4) + 1, jnp.int32)
        _lenS2 = 512 - jax.random.randint(jax.random.fold_in(_rk, 8), (8,), 0, max(1, 512 // 4) + 1, jnp.int32)
        _ctx_1024P = jax.random.normal(jax.random.fold_in(_rk, 11), (8, 16, 512), jnp.float32)
        _ctx_1024c = jax.random.dirichlet(jax.random.fold_in(_rk, 511), 0.3 * jnp.ones((16,), jnp.float32), (8, 512))
        _ctx_1024t = jnp.einsum('bsk,bkd->bsd', _ctx_1024c, _ctx_1024P)
        _ctx_1024t = _ctx_1024t * jax.lax.rsqrt(jnp.mean(jnp.square(_ctx_1024t)) + 1e-12) * 0.953939
        ctx_1024 = -1.39393e-06 + 0.999914 * (_ctx_1024t + 0.3 * jax.random.normal(jax.random.fold_in(_rk, 611), (8, 512, 512), jnp.float32))
        return (x, ctx_1024)
    x, ctx_1024 = _rec_inputs()

    def _L0_xattn_setup():
        import jax, jax.numpy as jnp
        import numpy as np
        D_MODEL = 512
        NUM_HEADS = 16
        HEAD_DIM = D_MODEL // NUM_HEADS

        def _split_heads(x):
            B, S, D = x.shape
            return x.reshape(B, S, NUM_HEADS, HEAD_DIM).transpose(0, 2, 1, 3)
        key = jax.random.key(seed)
        ks = jax.random.split(key, 11)
        B, S, D = (2, 1024, D_MODEL)
        scale = 1.0 / np.sqrt(D)
        inp = {'q': jax.random.normal(ks[0], (B, S, D), dtype=jnp.float32), 'k': jax.random.normal(ks[1], (B, S, D), dtype=jnp.float32), 'v': jax.random.normal(ks[2], (B, S, D), dtype=jnp.float32), 'Wq': jax.random.normal(ks[3], (D, D), dtype=jnp.float32) * scale, 'bq': jnp.zeros((D,), dtype=jnp.float32), 'Wk': jax.random.normal(ks[4], (D, D), dtype=jnp.float32) * scale, 'bk': jnp.zeros((D,), dtype=jnp.float32), 'Wv': jax.random.normal(ks[5], (D, D), dtype=jnp.float32) * scale, 'bv': jnp.zeros((D,), dtype=jnp.float32), 'Wo': jax.random.normal(ks[6], (D, D), dtype=jnp.float32) * scale, 'bo': jnp.zeros((D,), dtype=jnp.float32)}
        return inp
    _L0_xattn_all = _L0_xattn_setup()
    _L0_xattn_in = {k: v for k, v in _L0_xattn_all.items() if k in ('Wq', 'bq', 'Wk', 'bk', 'Wv', 'bv', 'Wo', 'bo')}
    del _L0_xattn_all

    def _L0_ffn_setup():
        import jax, jax.numpy as jnp
        import numpy as np
        D_MODEL, D_FF, RANK = (512, 2048, 128)
        B, S = (4, 2048)
        key = jax.random.key(seed)
        ks = jax.random.split(key, 7)
        return {'x': jax.random.normal(ks[0], (B, S, D_MODEL), dtype=jnp.float32), 'U1': jax.random.normal(ks[1], (D_MODEL, RANK), dtype=jnp.float32) * 0.02, 'V1': jax.random.normal(ks[2], (RANK, D_FF), dtype=jnp.float32) * 0.02, 'b1': jnp.zeros((D_FF,), dtype=jnp.float32), 'U2': jax.random.normal(ks[3], (D_FF, RANK), dtype=jnp.float32) * 0.02, 'V2': jax.random.normal(ks[4], (RANK, D_MODEL), dtype=jnp.float32) * 0.02, 'b2': jnp.zeros((D_MODEL,), dtype=jnp.float32)}
    _L0_ffn_all = _L0_ffn_setup()
    _L0_ffn_in = {k: v for k, v in _L0_ffn_all.items() if k in ('U1', 'V1', 'b1', 'U2', 'V2', 'b2')}
    del _L0_ffn_all
    return {'x': x, 'ctx_1024': ctx_1024, 'L0_xattn_Wq': _L0_xattn_in['Wq'], 'L0_xattn_bq': _L0_xattn_in['bq'], 'L0_xattn_Wk': _L0_xattn_in['Wk'], 'L0_xattn_bk': _L0_xattn_in['bk'], 'L0_xattn_Wv': _L0_xattn_in['Wv'], 'L0_xattn_bv': _L0_xattn_in['bv'], 'L0_xattn_Wo': _L0_xattn_in['Wo'], 'L0_xattn_bo': _L0_xattn_in['bo'], 'L0_ffn_U1': _L0_ffn_in['U1'], 'L0_ffn_V1': _L0_ffn_in['V1'], 'L0_ffn_b1': _L0_ffn_in['b1'], 'L0_ffn_U2': _L0_ffn_in['U2'], 'L0_ffn_V2': _L0_ffn_in['V2'], 'L0_ffn_b2': _L0_ffn_in['b2']}

def reference(x, ctx_1024, L0_xattn_Wq, L0_xattn_bq, L0_xattn_Wk, L0_xattn_bk, L0_xattn_Wv, L0_xattn_bv, L0_xattn_Wo, L0_xattn_bo, L0_ffn_U1, L0_ffn_V1, L0_ffn_b1, L0_ffn_U2, L0_ffn_V2, L0_ffn_b2):
    import jax
    import jax.numpy as jnp

    def _L0_xattn_ref(q, k, v, Wq, bq, Wk, bk, Wv, bv, Wo, bo):
        import jax, jax.numpy as jnp
        import numpy as np
        D_MODEL = 512
        NUM_HEADS = 16
        HEAD_DIM = D_MODEL // NUM_HEADS

        def _split_heads(x):
            B, S, D = x.shape
            return x.reshape(B, S, NUM_HEADS, HEAD_DIM).transpose(0, 2, 1, 3)
        B, S, D = q.shape
        qh = _split_heads(q @ Wq.T + bq)
        kh = _split_heads(k @ Wk.T + bk)
        vh = _split_heads(v @ Wv.T + bv)
        scores = jnp.einsum('bhqd,bhkd->bhqk', qh, kh) / jnp.sqrt(jnp.asarray(HEAD_DIM, dtype=qh.dtype))
        causal = jnp.tril(jnp.ones((S, S), dtype=bool))
        scores = jnp.where(causal[None, None], scores, -jnp.inf)
        attn = jax.nn.softmax(scores, axis=-1)
        out = jnp.einsum('bhqk,bhkd->bhqd', attn, vh)
        out = out.transpose(0, 2, 1, 3).reshape(B, S, D)
        return out @ Wo.T + bo

    def _L0_ffn_ref(x, U1, V1, b1, U2, V2, b2):
        import jax, jax.numpy as jnp
        import numpy as np
        D_MODEL, D_FF, RANK = (512, 2048, 128)
        B, S = (4, 2048)
        P = jnp.einsum('bsd,dr->bsr', x, U1)
        H = jax.nn.gelu(jnp.einsum('bsr,rf->bsf', P, V1) + b1)
        Q = jnp.einsum('bsf,fr->bsr', H, U2)
        return jnp.einsum('bsr,rd->bsd', Q, V2) + b2
    x = x + _L0_xattn_ref(_layernorm(x, axis=-1), ctx_1024, ctx_1024, L0_xattn_Wq, L0_xattn_bq, L0_xattn_Wk, L0_xattn_bk, L0_xattn_Wv, L0_xattn_bv, L0_xattn_Wo, L0_xattn_bo)
    x = x + _L0_ffn_ref(_layernorm(x, axis=-1), L0_ffn_U1, L0_ffn_V1, L0_ffn_b1, L0_ffn_U2, L0_ffn_V2, L0_ffn_b2)
    return x

_drawn_inputs = setup_inputs


def setup_inputs(seed=0):
    import zlib

    import numpy as np

    out = dict(_drawn_inputs(seed))
    spreads = {'L0_xattn_bq': (0.0, 0.402),
     'L0_xattn_bk': (0.0, 2.0),
     'L0_xattn_bv': (0.0, 0.1),
     'L0_xattn_bo': (0.0, 0.1),
     'L0_ffn_b1': (0.0, 0.8),
     'L0_ffn_b2': (0.0, 0.8)}
    factors = {'L0_ffn_U1': 6.204, 'L0_ffn_V1': 6.204, 'L0_ffn_U2': 4.451, 'L0_ffn_V2': 4.654}
    for name, (base, spread) in spreads.items():
        noise = np.random.default_rng([zlib.crc32(name.encode()), seed]).standard_normal(out[name].shape)
        drawn = base * np.exp(spread * noise) if base else spread * noise
        out[name] = jnp.asarray(drawn.astype(out[name].dtype))
    for name, factor in factors.items():
        out[name] = (out[name] * factor).astype(out[name].dtype)
    return out
```

```python
import concourse.bass as bass
from concourse import mybir
from contextlib import ExitStack

FP32 = mybir.dt.float32
F32R = mybir.dt.float32r
BF16 = mybir.dt.bfloat16
ALU = mybir.AluOpType
ACT = mybir.ActivationFunctionType
AXIS_X = mybir.AxisListType.X

B, S, D = 8, 512, 512
P = 128
H, HD = 16, 32
NT = S // P
NK = D // P
HG = P // HD
NG = H // HG
FF, R = 2048, 128
NF = FF // P
EPS = 1e-5
SCALE = 1.0 / (HD ** 0.5)
MASKED = -3.0e38
UNITS = 10
A_UNITS, B_UNITS = HG, HG

TERMS = ((0, 0), (0, 1), (1, 0))


def wait_apart(eng, met, count, sem, value):
    if not isinstance(value, int):
        value = eng.to_reg(value)
    eng.wait_ge(met, count)
    eng.wait_ge(sem, value)


def attention_phase(nc, x, ctx_in, Wq, bq, Wk, bk, Wv, bv, Wo, bo, x1_dram):
    with ExitStack() as ctx:
        def sb(name, shape, dt=FP32):
            return ctx.enter_context(nc.sbuf_tensor(name, shape, dt))

        def sem(name):
            return ctx.enter_context(nc.semaphore(name))

        wqT = sb("wqT", [P, 2, NK, D], F32R)
        wkT = sb("wkT", [P, 2, NK, D], F32R)
        wvT = sb("wvT", [P, 2, NK, D], F32R)
        woT = sb("woT", [P, 2, NK, D], F32R)
        xnT = sb("xnT", [P, 2, NK, S], F32R)
        cxT = sb("cxT", [P, 2, NK, S], F32R)
        attnT = sb("attnT", [P, 2, NK, S], F32R)
        QLO, QHI, KHI, KLO = range(4)
        qk = sb("qk", [P, 4, S], F32R)
        M_ROW = 3 * HD
        qs = sb("qs", [P, 2, 2, HG, S], F32R)
        v = sb("v", [P, NT, D])
        probs = sb("probs", [P, UNITS, S])
        xbuf = sb("xbuf", [P, NT, D])
        cbuf = sb("cbuf", [P, NT, D])
        attn = sb("attn", [P, S])
        mrow = sb("mrow", [HG, 2, S], F32R)
        negmax = sb("negmax", [P, NT, HG])
        bo_all = sb("bo_all", [P, D])
        ident = sb("ident", [P, P])
        ident16 = sb("ident16", [P, P], BF16)
        mask16 = sb("mask16", [P, P], BF16)
        ones32 = sb("ones32", [P, HD])
        ones_row = sb("ones_row", [1, P])
        bqc = sb("bqc", [P, NK])
        bkc = sb("bkc", [P, NK])
        bvc = sb("bvc", [P, NK])
        stats = sb("stats", [P, NT, 6])
        mv = sb("mv", [P, NT, 2])
        rstd = sb("rstd", [P, NT])
        varp = sb("varp", [P, NT])
        minus_half = sb("minus_half", [P, NT])

        psum = [ctx.enter_context(nc.psum_tensor(f"ps{i}", [P, 512], FP32)) for i in range(8)]
        score_ps, max_ps, gen_ps, out_ps, den_ps = psum[0:2], psum[2:4], psum[4:6], psum[6], psum[7]

        w_loaded = [sem(f"w_loaded{i}") for i in range(4)]
        small_loaded = sem("small_loaded")
        bo_loaded = sem("bo_loaded")
        const_made = sem("const_made")
        const_step = sem("const_step")
        x_loaded = sem("x_loaded")
        ctx_loaded = sem("ctx_loaded")
        gen_ready = sem("gen_ready")
        rounded = sem("rounded")
        evacuated = sem("evacuated")
        stacked = sem("stacked")
        m_stacked = sem("m_stacked")
        max_ready = sem("max_ready")
        max_done = sem("max_done")
        score_ready = sem("score_ready")
        exp_done = sem("exp_done")
        masked = sem("masked")
        folded = sem("folded")
        av0_done = sem("av0_done")
        av_done = sem("av_done")
        recip_done = sem("recip_done")
        attn_scaled = sem("attn_scaled")
        attn_rounded = sem("attn_rounded")
        attn_ready = sem("attn_ready")
        stats_done = sem("stats_done")
        mv_done = sem("mv_done")
        var_done = sem("var_done")
        rstd_done = sem("rstd_done")
        normed = sem("normed")
        residual_ready = sem("residual_ready")
        x1_stored = sem("x1_stored")

        def in_step(last):
            uses = []
            for g in range(NG):
                if not (last and g >= 2):
                    uses += [("q", g), ("k", g)]
                if not (last and g == NG - 1):
                    uses.append(("m", g))
                if g == 1 and not last:
                    uses += [("c", t) for t in range(NT)] + [("x", t) for t in range(NT)]
                if g == NG - 1:
                    if not last:
                        uses += [("v", t) for t in range(NT)]
                    uses += [("o", t) for t in range(NT)]
            return uses

        first = [("w", i, k) for i in range(4) for k in range(NK)] + [("bo",)]
        first += [("c", t) for t in range(NT)] + [("x", t) for t in range(NT)]
        first += [("q", -2), ("k", -2), ("q", -1), ("k", -1)] + [("v", t) for t in range(NT)] + [("m", -1)]
        SPLIT = "wcxqkm"
        PER_STEP = len(in_step(False))
        SPLITS = sum(u[0] in SPLIT for u in in_step(False))
        assert len(first) % 2 == 0 and PER_STEP % 2 == 0

        def use(b, last, key):
            if b is None:
                return first.index(key)
            return b * PER_STEP + (len(first) + in_step(last).index(key))

        def split(b, last, key):
            def count(l):
                return sum(u[0] in SPLIT for u in l[:l.index(key)])
            if b is None:
                return count(first)
            return b * SPLITS + (sum(u[0] in SPLIT for u in first) + count(in_step(last)))

        def bank(b, last, key):
            l = first if b is None else in_step(last)
            return gen_ps[l.index(key) % 2]

        def unit(u):
            if u < A_UNITS:
                return "A", u
            if u < A_UNITS + B_UNITS:
                return "B", u - A_UNITS
            return "C", u - A_UNITS - B_UNITS

        K_LO, K_MID, K_HI = P, 2 * P, 3 * P

        block = ctx.enter_context(nc.Block())

        @block.sync
        def _(sp):
            weights = [(Wq, probs[:, 0:NK, :]), (Wk, probs[:, NK:2 * NK, :]), (Wv, v[:, :, :]),
                       (Wo, probs[:, 0:NK, :])]

            def load_weight(i):
                w, to = weights[i]
                sp.dma_start(to, w.rearrange("(m p) n -> p m n", p=P)).then_inc(w_loaded[i], 16)

            def load_tokens(to, of, b, loaded):
                sp.dma_start(to[:, :, :], of[bass.ds(b, 1), :, :].rearrange("a (t p) d -> p (a t) d", p=P)).then_inc(loaded, 16)

            def stack(n, slot):
                for h in range(HG):
                    rows = slice(h * HD, (h + 1) * HD)
                    for row, pair in enumerate((slice(QHI, KHI + 1), slice(QLO, KHI + 1, 2), slice(QHI, KLO + 1, 2))):
                        sp.dma_start(qs[row * HD:(row + 1) * HD, slot, :, h, :].bitcast(FP32),
                                     qk[rows, pair, :].bitcast(FP32)).then_inc(stacked, 16)

            def stack_max(slot):
                sp.dma_start(qs[M_ROW:M_ROW + 1, slot, 0, :, :].bitcast(FP32),
                             mrow[:, 0, :].bitcast(FP32)).then_inc(m_stacked, 16)
                sp.dma_start(qs[M_ROW + 1:M_ROW + 2, slot, 0, :, :].bitcast(FP32),
                             mrow[:, 1, :].bitcast(FP32)).then_inc(m_stacked, 16)

            load_weight(0)
            load_weight(1)
            load_weight(2)
            load_tokens(cbuf, ctx_in, 0, ctx_loaded)
            load_tokens(xbuf, x, 0, x_loaded)
            for b_, c in ((bq, bqc), (bk, bkc), (bv, bvc)):
                sp.dma_start(c[:, :], b_.rearrange("(m p) -> p m", p=P), allow_slow_non_contiguous=True).then_inc(small_loaded, 16)
            sp.dma_start(attn[0:1, :], bo.rearrange("(a n) -> a n", a=1)).then_inc(bo_loaded, 16)
            sp.wait_ge(gen_ready, use(None, False, ("w", 0, NK - 1)) + 1)
            load_weight(3)
            sp.wait_ge(const_made, 1)
            for n in (0, 1):
                sp.wait_ge(evacuated, use(None, False, ("k", n - 2)) + 1)
                stack(n, n)
            sp.wait_ge(evacuated, use(None, False, ("m", -1)) + 1)
            stack_max(0)

            def step(b, last):
                if not last:
                    if isinstance(b, int) and b == 0:
                        sp.wait_ge(gen_ready, use(None, False, ("x", NT - 1)) + 1)
                    else:
                        sp.wait_ge(x1_stored, b * 64)
                    load_tokens(xbuf, x, b + 1, x_loaded)
                    load_tokens(cbuf, ctx_in, b + 1, ctx_loaded)
                for g in range(NG):
                    if g == 2:
                        if not last:
                            sp.wait_ge(gen_ready, use(b, last, ("x", NT - 1)) + 1)
                        else:
                            sp.wait_ge(x1_stored, b * 64)
                        load_tokens(xbuf, x, b, x_loaded)
                    if not (last and g >= 2):
                        wait_apart(sp, const_made, 1, evacuated, use(b, last, ("k", g)) + 1)
                        sp.wait_ge(score_ready, b * (NG * UNITS) + UNITS * (g + 1))
                        stack(None, g % 2)
                    if not (last and g == NG - 1):
                        sp.wait_ge(evacuated, use(b, last, ("m", g)) + 1)
                        stack_max((g + 1) % 2)
                for t in range(NT):
                    sp.wait_ge(evacuated, use(b, last, ("o", t)) + 1)
                    sp.dma_start(x1_dram[bass.ds(b, 1), t * P:(t + 1) * P, :].rearrange("a p d -> (a p) d"),
                                 xbuf[:, t, :]).then_inc(x1_stored, 16)

            step(0, False)
            with sp.Fori(1, B - 1) as b:
                step(b, False)
            step(B - 1, True)
            sp.wait_ge(x1_stored, 64 * B)

        @block.gpsimd
        def _(pool):
            pool.memset(ident[:, :], 0.0).then_inc(const_step, 1)
            pool.memset(mask16[:, :], 0.0).then_inc(const_step, 1)
            pool.memset(ones32[:, :], 1.0).then_inc(const_step, 1)
            pool.memset(ones_row[:, :], 1.0).then_inc(const_step, 1)
            pool.memset(minus_half[:, :], -0.5).then_inc(const_step, 1)
            pool.wait_ge(const_step, 5)
            pool.memset(qs[M_ROW:P, :, :, :, :].bitcast(FP32), 0.0).then_inc(const_step, 1)
            pool.wait_ge(const_step, 6)
            pool.affine_select(out=ident[:, :], in_=ident[:, :], compare_op=ALU.not_equal, fill=1.0,
                               base=0, pattern=[[-1, P]], channel_multiplier=1).then_inc(const_step, 1)
            pool.affine_select(out=mask16[:, :], in_=mask16[:, :], compare_op=ALU.is_ge, fill=MASKED,
                               base=0, pattern=[[-1, P]], channel_multiplier=1).then_inc(const_step, 1)
            pool.wait_ge(const_step, 8)
            pool.memset(qs[M_ROW:M_ROW + 2, :, 1, :, :].bitcast(FP32), 1.0).then_inc(const_step, 1)
            pool.wait_ge(const_step, 9)
            pool.tensor_copy(ident16[:, :], ident[:, :]).then_inc(const_made, 1)

            def rstds(done):
                wait_apart(pool, const_step, 3, mv_done, done * NT + NT)
                pool.tensor_scalar(varp[:, :], mv[:, :, 1], EPS, None, ALU.add).then_inc(var_done, 1)
                pool.wait_ge(var_done, done + 1)
                pool.tensor_tensor(rstd[:, :], varp[:, :], minus_half[:, :], ALU.pow).then_inc(rstd_done, 1)

            rstds(0)

            def causal(view):
                pool.affine_select(out=view, in_=view, compare_op=ALU.is_ge, fill=0.0, base=0,
                                   pattern=[[0, HG], [1, P]], channel_multiplier=-1).then_inc(masked, 1)

            pa, pb, pc = probs[:, 0:HG, :], probs[:, HG:2 * HG, :], probs[:, 2 * HG:UNITS, :]
            pc4 = pc.rearrange("p c (h q) -> p (c h) q", h=2)

            def step(b, last):
                for g in range(NG):
                    grp = b * NG + g
                    units = b * (NG * UNITS) + g * UNITS
                    wait_apart(pool, const_step, 9, exp_done, units + A_UNITS)
                    causal(pa[:, :, 0:P])
                    wait_apart(pool, const_step, 9, exp_done, units + A_UNITS + B_UNITS)
                    causal(pb[:, :, 0:P])
                    causal(pb[:, :, K_HI:S])
                    wait_apart(pool, const_step, 9, exp_done, units + UNITS)
                    causal(pc4[:, :, 0:P])
                    pool.wait_ge(av0_done, grp + 1)
                    pool.wait_ge(masked, grp * 4 + 4)
                    pool.tensor_tensor(pa[:, :, K_LO:S], pa[:, :, K_LO:S], pb[:, :, 0:S - K_LO], ALU.add).then_inc(folded, 1)
                    pool.wait_ge(folded, grp * 3 + 1)
                    pool.tensor_tensor(pa[:, :, K_MID:S], pa[:, :, K_MID:S], pc4, ALU.add).then_inc(folded, 1)
                    pool.wait_ge(folded, grp * 3 + 2)
                    pool.tensor_tensor(pa[:, :, K_HI:S], pa[:, :, K_HI:S], pb[:, :, K_HI:S], ALU.add).then_inc(folded, 1)
                    if g == 0 and not last:
                        rstds(b + 1)
                    if g == 2:
                        pool.wait_ge(x_loaded, b * 32 + (48 if not last else 32))
                        pool.wait_ge(evacuated, use(None, False, ("bo",)) + 1)
                        for t in range(NT):
                            pool.tensor_tensor(xbuf[:, t, :], xbuf[:, t, :], bo_all[:, :], ALU.add).then_inc(residual_ready, 1)

            step(0, False)
            with pool.Fori(1, B - 1) as b:
                step(b, False)
            step(B - 1, True)

        @block.scalar
        def _(act):
            def hi(out, b, last, key, bias=None):
                act.wait_ge(gen_ready, use(b, last, key) + 1)
                ps = bank(b, last, key)
                if key[0] in "cx":
                    ps = ps[:, :].rearrange("p (k t) -> p k t", k=NK)
                elif key[0] == "m":
                    ps = ps[0:HG, :]
                else:
                    ps = ps[:, :]
                if bias is None:
                    nc.scalar.activation(out, ps, ACT.Copy).then_inc(rounded, 1)
                else:
                    nc.scalar.activation(out, ps, ACT.Identity, bias=bias).then_inc(rounded, 1)

            def tokens_hi(b, last):
                for t in range(NT):
                    hi(cxT[:, 0, :, t * P:(t + 1) * P], b, last, ("c", t))
                for t in range(NT):
                    hi(xnT[:, 0, :, t * P:(t + 1) * P], b, last, ("x", t))

            for i, w in enumerate((wqT, wkT, wvT, woT)):
                for k in range(NK):
                    hi(w[:, 0, k, :], None, False, ("w", i, k))
            tokens_hi(None, False)
            act.wait_ge(small_loaded, 48)
            for g in (-2, -1):
                if g == -1:
                    act.wait_ge(stacked, 192)
                hi(qk[:, QHI, :], None, False, ("q", g), bqc[:, g + 2:g + 3])
                hi(qk[:, KHI, :], None, False, ("k", g), bkc[:, g + 2:g + 3])
            hi(mrow[:, 0, :], None, False, ("m", -1))

            def step(b, last):
                for g in range(NG):
                    grp = b * NG + g
                    units = b * (NG * UNITS) + g * UNITS
                    project = not (last and g >= 2)
                    for u in range(UNITS):
                        act.wait_ge(score_ready, units + u + 1)
                        nc.scalar.activation(probs[:, u, :], score_ps[u % 2][:, :], ACT.Exp, scale=SCALE).then_inc(exp_done, 1)
                        if u == 6 and project:
                            act.wait_ge(stacked, (grp + 2) * 192)
                            mt = (g + 2) % NG
                            hi(qk[:, QHI, :], b, last, ("q", g), bqc[:, mt:mt + 1])
                    if project:
                        hi(qk[:, KHI, :], b, last, ("k", g), bkc[:, mt:mt + 1])
                    if not (last and g == NG - 1):
                        act.wait_ge(m_stacked, (grp + 1) * 32)
                        hi(mrow[:, 0, :], b, last, ("m", g))
                    act.wait_ge(attn_scaled, grp + 1)
                    nc.scalar.activation(attnT[:, 0, g, :], attn[:, :], ACT.Identity, bias=bvc[:, g:g + 1]).then_inc(attn_rounded, 1)
                    if g == 1 and not last:
                        tokens_hi(b, last)

            step(0, False)
            with act.Fori(1, B - 1) as b:
                step(b, False)
            step(B - 1, True)

        @block.vector
        def _(dve):
            def lo(out, hi_half, b, last, key, bias=None):
                dve.wait_ge(rounded, split(b, last, key) + 1)
                ps = bank(b, last, key)
                if key[0] in "cx":
                    ps = ps[:, :].rearrange("p (k t) -> p k t", k=NK)
                elif key[0] == "m":
                    ps = ps[0:HG, :]
                else:
                    ps = ps[:, :]
                hi_half = hi_half.bitcast(FP32)
                if bias is None:
                    nc.vector.tensor_tensor(out, ps, hi_half, ALU.subtract).then_inc(evacuated, 1)
                else:
                    nc.vector.scalar_tensor_tensor(out, ps, bias, hi_half, ALU.add, ALU.subtract).then_inc(evacuated, 1)

            def norm_stats(done):
                for t in range(NT):
                    nc.vector.bn_stats(stats[:, t, :], xbuf[:, t, :]).then_inc(stats_done, 1)
                for t in range(NT):
                    wait_apart(dve, const_made, 1, stats_done, done * NT + t + 1)
                    nc.vector.bn_aggr(mv[:, t, :], stats[:, t, :]).then_inc(mv_done, 1)

            def normalise(done):
                dve.wait_ge(rstd_done, done + 1)
                for t in range(NT):
                    nc.vector.tensor_scalar(xbuf[:, t, :], xbuf[:, t, :], mv[:, t, 0:1], rstd[:, t:t + 1],
                                            ALU.subtract, ALU.mult).then_inc(normed, 1)

            def tokens_lo(b, last):
                for name, to in (("c", cxT), ("x", xnT)):
                    for t in range(NT):
                        cols = slice(t * P, (t + 1) * P)
                        lo(to[:, 1, :, cols], to[:, 0, :, cols], b, last, (name, t))

            def maxima(n_units, u):
                dve.wait_ge(max_ready, n_units + u + 1)
                kind, j = unit(u)
                ps = max_ps[u % 2]

                def take(out, in_):
                    return nc.vector.tensor_reduce(out, in_, AXIS_X, ALU.max, negate=True)

                if kind == "A":
                    take(negmax[:, 3, j:j + 1], ps[:, :]).then_inc(max_done, 1)
                elif kind == "B":
                    take(negmax[:, 0, j:j + 1], ps[:, 0:P])
                    take(negmax[:, 2, j:j + 1], ps[:, P:S]).then_inc(max_done, 1)
                else:
                    take(negmax[:, 1, 2 * j:2 * j + 2], ps[:, :].rearrange("p (h k) -> p h k", h=2)).then_inc(max_done, 1)

            for i, w in enumerate((wqT, wkT, wvT, woT)):
                for k in range(NK):
                    lo(w[:, 1, k, :], w[:, 0, k, :], None, False, ("w", i, k))
            dve.wait_ge(gen_ready, use(None, False, ("bo",)) + 1)
            nc.vector.tensor_copy(bo_all[:, :], bank(None, False, ("bo",))[:, :]).then_inc(evacuated, 1)
            dve.wait_ge(x_loaded, 16)
            norm_stats(0)
            normalise(0)
            tokens_lo(None, False)
            dve.wait_ge(small_loaded, 48)
            for g in (-2, -1):
                lo(qk[:, QLO, :], qk[:, QHI, :], None, False, ("q", g), bqc[:, g + 2:g + 3])
                lo(qk[:, KLO, :], qk[:, KHI, :], None, False, ("k", g), bkc[:, g + 2:g + 3])

            def values(b, last):
                for t in range(NT):
                    dve.wait_ge(gen_ready, use(b, last, ("v", t)) + 1)
                    nc.vector.tensor_copy(v[:, t, :], bank(b, last, ("v", t))[:, :]).then_inc(evacuated, 1)

            values(None, False)
            for u in range(UNITS):
                maxima(0, u)
            lo(mrow[:, 1, :], mrow[:, 0, :], None, False, ("m", -1))

            def step(b, last):
                for g in range(NG):
                    grp = b * NG + g
                    project = not (last and g >= 2)
                    mt = (g + 2) % NG
                    for u in range(UNITS):
                        if not (last and g == NG - 1):
                            maxima(b * (NG * UNITS) + (g + 1) * UNITS, u)
                        if u == 6 and project:
                            lo(qk[:, QLO, :], qk[:, QHI, :], b, last, ("q", g), bqc[:, mt:mt + 1])
                    if project:
                        lo(qk[:, KLO, :], qk[:, KHI, :], b, last, ("k", g), bkc[:, mt:mt + 1])
                    if not (last and g == NG - 1):
                        lo(mrow[:, 1, :], mrow[:, 0, :], b, last, ("m", g))
                    if g == 0 and not last:
                        dve.wait_ge(x_loaded, b * 32 + 32)
                        norm_stats(b + 1)
                    if not (isinstance(b, int) and b == 0 and g == 0):
                        dve.wait_ge(attn_ready, grp)
                    dve.wait_ge(av_done, grp + 1)
                    nc.vector.reciprocal(attn[:, :], den_ps[:, :]).then_inc(recip_done, 1)
                    dve.wait_ge(recip_done, grp + 1)
                    nc.vector.tensor_tensor(attn[:, :], out_ps[:, :], attn[:, :], ALU.mult).then_inc(attn_scaled, 1)
                    if g == 1 and not last:
                        normalise(b + 1)
                    dve.wait_ge(attn_rounded, grp + 1)
                    nc.vector.scalar_tensor_tensor(attnT[:, 1, g, :], attn[:, :], bvc[:, g:g + 1],
                                                   attnT[:, 0, g, :].bitcast(FP32), ALU.add, ALU.subtract).then_inc(attn_ready, 1)
                    if g == 1 and not last:
                        tokens_lo(b, last)
                if not last:
                    values(b, last)
                for t in range(NT):
                    dve.wait_ge(gen_ready, use(b, last, ("o", t)) + 1)
                    dve.wait_ge(residual_ready, b * NT + t + 1)
                    nc.vector.tensor_tensor(xbuf[:, t, :], bank(b, last, ("o", t))[:, :], xbuf[:, t, :], ALU.add).then_inc(evacuated, 1)

            step(0, False)
            with dve.Fori(1, B - 1) as b:
                step(b, False)
            step(B - 1, True)

        @block.tensor
        def _(pe):
            def claim(b, last, key):
                n = use(b, last, key)
                if b is not None or n >= 2:
                    pe.wait_ge(evacuated, n - 1)
                return bank(b, last, key)

            def transposed(b, last, key, of):
                ps = claim(b, last, key)
                for k in range(4):
                    done = nc.tensor.transpose(ps[:, k * P:(k + 1) * P], of(k), ident[:, :])
                done.then_inc(gen_ready, 1)

            def product(ps, pairs):
                todo = [(k, i, j) for k in range(NK) for i, j in TERMS]

                def issue(n):
                    k, i, j = todo[n]
                    left, right = pairs(k, i, j)
                    return nc.tensor.matmul(ps[:, :], left, right, start=(n == 0), stop=(n == len(todo) - 1))
                return len(todo), issue

            def q_product(ps, mt):
                return product(ps, lambda k, i, j: (wqT[:, i, k, mt * P:(mt + 1) * P], xnT[:, j, k, :]))

            def k_product(ps, mt):
                return product(ps, lambda k, i, j: (wkT[:, i, k, mt * P:(mt + 1) * P], cxT[:, j, k, :]))

            def whole(b, last, key, make):
                ps = claim(b, last, key)
                n, issue = make(ps)
                for i in range(n):
                    done = issue(i)
                done.then_inc(gen_ready, 1)

            def values(b, last):
                for t in range(NT):
                    whole(b, last, ("v", t), lambda ps: product(
                        ps, lambda k, i, j: (cxT[:, i, k, t * P:(t + 1) * P], wvT[:, j, k, :])))

            def max_unit(units, slot, u):
                if isinstance(units, int) and units + u < 2:
                    pass
                else:
                    pe.wait_ge(max_done, units + u - 1)
                kind, j = unit(u)
                ps = max_ps[u % 2]

                def scores(h, qt, c0, c1):
                    nc.tensor.matmul(ps[:, c0:c1], qs[0:M_ROW, slot, 0, h, qt * P:(qt + 1) * P],
                                     qs[0:M_ROW, slot, 1, h, 0:c1 - c0], start=True, stop=False)

                def mask(c):
                    return nc.tensor.matmul(ps[:, c:c + P], ident16[:, :], mask16[:, :], start=False, stop=True)

                if kind == "A":
                    scores(j, 3, 0, S)
                    done = mask(3 * P)
                elif kind == "B":
                    scores(j, 0, 0, 2 * P)
                    mask(0)
                    scores(j, 2, P, S)
                    done = mask(3 * P)
                else:
                    for i in range(2):
                        scores(2 * j + i, 1, i * 2 * P, (i + 1) * 2 * P)
                        done = mask((2 * i + 1) * P)
                done.then_inc(max_ready, 1)

            def score_unit(units, slot, u):
                if not (isinstance(units, int) and units + u < 2):
                    pe.wait_ge(exp_done, units + u - 1)
                kind, j = unit(u)
                ps = score_ps[u % 2]

                def scores(h, kt, q0, c0, c1):
                    return nc.tensor.matmul(ps[:, c0:c1], qs[:, slot, 1, h, kt * P:(kt + 1) * P],
                                            qs[:, slot, 0, h, q0:q0 + c1 - c0], start=True, stop=True)

                if kind == "A":
                    done = scores(j, 0, 0, 0, S)
                elif kind == "B":
                    scores(j, 3, 2 * P, 2 * P, S)
                    done = scores(j, 1, P, 0, 3 * P)
                else:
                    scores(2 * j, 2, 2 * P, 0, 2 * P)
                    done = scores(2 * j + 1, 2, 2 * P, 2 * P, S)
                done.then_inc(score_ready, 1)

            def weigh(g, kt, of):
                for h in range(HG):
                    done = nc.tensor.matmul(out_ps[h * HD:(h + 1) * HD, kt * P:S],
                                            v[:, kt, g * P + h * HD:g * P + (h + 1) * HD], of(h),
                                            start=(kt == 0), stop=(kt == 2))
                return done

            pe.wait_ge(const_made, 1)
            for i, w in enumerate((probs[:, 0:NK, :], probs[:, NK:2 * NK, :], v[:, :, :], probs[:, 0:NK, :])):
                pe.wait_ge(w_loaded[i], 16)
                for k in range(NK):
                    transposed(None, False, ("w", i, k), lambda m: w[:, m, k * P:(k + 1) * P])
            ps = claim(None, False, ("bo",))
            pe.wait_ge(bo_loaded, 16)
            nc.tensor.matmul(ps[:, :], ones_row[:, :], attn[0:1, :], start=True, stop=True).then_inc(gen_ready, 1)
            pe.wait_ge(ctx_loaded, 16)
            for t in range(NT):
                transposed(None, False, ("c", t), lambda k: cbuf[:, t, k * P:(k + 1) * P])
            for t in range(NT):
                pe.wait_ge(normed, t + 1)
                transposed(None, False, ("x", t), lambda k: xbuf[:, t, k * P:(k + 1) * P])
            pe.wait_ge(evacuated, use(None, False, ("x", NT - 1)) + 1)
            for g in (-2, -1):
                whole(None, False, ("q", g), lambda ps: q_product(ps, g + 2))
                whole(None, False, ("k", g), lambda ps: k_product(ps, g + 2))
            values(None, False)
            pe.wait_ge(stacked, 192)
            for u in range(UNITS):
                max_unit(0, 0, u)
            pe.wait_ge(max_done, UNITS)
            ps = claim(None, False, ("m", -1))
            for t in range(NT):
                done = nc.tensor.transpose(ps[0:HG, t * P:(t + 1) * P], negmax[:, t, :], ident[:, :])
            done.then_inc(gen_ready, 1)

            def step(b, last):
                pa, pb, pc = probs[:, 0:HG, :], probs[:, HG:2 * HG, :], probs[:, 2 * HG:UNITS, :]
                for g in range(NG):
                    grp = b * NG + g
                    units = b * (NG * UNITS) + g * UNITS
                    project = not (last and g >= 2)
                    ahead = not (last and g == NG - 1)
                    mt = (g + 2) % NG
                    pe.wait_ge(m_stacked, grp * 32 + 32)
                    if project:
                        if g == 2:
                            pe.wait_ge(evacuated, use(b, last, ("x", NT - 1)) + 1)
                        nq, q_issue = q_product(claim(b, last, ("q", g)), mt)
                    issued = 0
                    for u in range(UNITS):
                        score_unit(units, g % 2, u)
                        if ahead:
                            if u == 0:
                                pe.wait_ge(stacked, (grp + 2) * 192)
                            max_unit(units + UNITS, (g + 1) % 2, u)
                        if project:
                            if u == 5:
                                nk, k_issue = k_product(claim(b, last, ("k", g)), mt)
                            until = (u + 1) * (nq + nk if u >= 5 else 2 * nq) // UNITS
                            for i in range(issued, until):
                                done = q_issue(i) if i < nq else k_issue(i - nq)
                                if i == nq - 1 or i == nq + nq - 1:
                                    done.then_inc(gen_ready, 1)
                            issued = until
                        if u == 7:
                            pe.wait_ge(masked, grp * 4 + 1)
                            pe.wait_ge(evacuated, use(b - 1, False, ("v", NT - 1)) + 1
                                       if not (isinstance(b, int) and b == 0) else use(None, False, ("v", NT - 1)) + 1)
                            if not (isinstance(b, int) and b == 0 and g == 0):
                                pe.wait_ge(attn_scaled, grp)
                            weigh(g, 0, lambda h: pa[:, h, :]).then_inc(av0_done, 1)
                    if ahead:
                        pe.wait_ge(max_done, units + 2 * UNITS)
                        ps = claim(b, last, ("m", g))
                        for t in range(NT):
                            done = nc.tensor.transpose(ps[0:HG, t * P:(t + 1) * P], negmax[:, t, :], ident[:, :])
                        done.then_inc(gen_ready, 1)
                    pe.wait_ge(masked, grp * 4 + 3)
                    weigh(g, 1, lambda h: pb[:, h, 0:S - K_LO])
                    weigh(g, 3, lambda h: pb[:, h, K_HI:S])
                    pe.wait_ge(masked, grp * 4 + 4)
                    weigh(g, 2, lambda h: pc[:, h // 2, (h % 2) * K_MID:(h % 2 + 1) * K_MID])
                    pe.wait_ge(folded, grp * 3 + 3)
                    for h in range(HG):
                        done = nc.tensor.matmul(den_ps[h * HD:(h + 1) * HD, :], ones32[:, :], pa[:, h, :], start=True, stop=True)
                    done.then_inc(av_done, 1)
                    if g == 1 and not last:
                        pe.wait_ge(ctx_loaded, b * 16 + 32)
                        for t in range(NT):
                            transposed(b, last, ("c", t), lambda k: cbuf[:, t, k * P:(k + 1) * P])
                        for t in range(NT):
                            pe.wait_ge(normed, b * NT + (NT + t + 1))
                            transposed(b, last, ("x", t), lambda k: xbuf[:, t, k * P:(k + 1) * P])
                if not last:
                    values(b, last)
                pe.wait_ge(attn_ready, b * NG + NG)
                for t in range(NT):
                    whole(b, last, ("o", t), lambda ps: product(
                        ps, lambda k, i, j: (attnT[:, i, k, t * P:(t + 1) * P], woT[:, j, k, :])))

            step(0, False)
            with pe.Fori(1, B - 1) as b:
                step(b, False)
            step(B - 1, True)


def ffn_phase(nc, x1_dram, U1, V1, b1, U2, V2, b2, out):
    with ExitStack() as ctx:
        def sb(name, shape, dt=FP32):
            return ctx.enter_context(nc.sbuf_tensor(name, shape, dt))

        def sem(name):
            return ctx.enter_context(nc.semaphore(name))

        RING = 4
        LAG = 3
        GENS = 3

        u1 = sb("u1", [P, 2, NK, R], F32R)
        v1 = sb("v1", [P, 2, FF], F32R)
        u2 = sb("u2", [P, 2, NF, R], F32R)
        v2 = sb("v2", [P, 2, D], F32R)
        u1_raw = sb("u1_raw", [P, NK, R])
        v1_raw = sb("v1_raw", [P, FF])
        u2_raw = sb("u2_raw", [P, NF, R])
        v2_raw = sb("v2_raw", [P, D])
        b1c = sb("b1c", [P, NF])
        b2_row = sb("b2_row", [1, D])
        b2_all = sb("b2_all", [P, D])
        ones_row = sb("ones_row2", [1, P])
        ident = sb("ident2", [P, P])
        xa = sb("xa", [P, NT, D])
        xn = sb("xn", [P, NT, D])
        y = sb("y", [P, NT, D])
        xnT = sb("xn2T", [P, 2, NK, S], F32R)
        pT = sb("pT", [P, 2, S], F32R)
        qT = sb("qT", [P, 2, S], F32R)
        gelu = sb("gelu", [P, RING, S])
        hT = sb("hT", [P, RING, 2, S], F32R)
        stats = sb("stats2", [P, NT, 6])
        mv = sb("mv2", [P, NT, 2])
        rstd = sb("rstd2", [P, NT])
        varp = sb("varp2", [P, NT])
        minus_half = sb("minus_half2", [P, NT])

        psum = [ctx.enter_context(nc.psum_tensor(f"psf{i}", [P, 512], FP32)) for i in range(8)]
        h_ps, gen_ps, q_ps = psum[0:RING], psum[RING:RING + GENS], psum[7]

        w_loaded = [sem(f"f_w_loaded{i}") for i in range(4)]
        small_loaded = sem("f_small_loaded")
        const_step = sem("f_const_step")
        const_made = sem("f_const_made")
        x_loaded = sem("f_x_loaded")
        w_rounded = sem("w_rounded")
        w_split = sem("w_split")
        gen_ready = sem("f_gen_ready")
        rounded = sem("f_rounded")
        evacuated = sem("f_evacuated")
        h_ready = sem("h_ready")
        gelu_done = sem("gelu_done")
        h_rounded = sem("h_rounded")
        h_split = sem("h_split")
        h_used = sem("h_used")
        q_rounded = sem("q_rounded")
        q_split = sem("q_split")
        stats_done = sem("f_stats_done")
        mv_done = sem("f_mv_done")
        var_done = sem("f_var_done")
        rstd_done = sem("f_rstd_done")
        normed = sem("f_normed")
        y_ready = sem("y_ready")
        stored = sem("stored")

        FIRST = ["b2"] + [("x", t) for t in range(NT)] + ["p"]
        STEP = [("x", t) for t in range(NT)] + ["p"] + [("o", t) for t in range(NT)]
        assert len(FIRST) % GENS == 0 and len(STEP) % GENS == 0
        LAST = [("o", t) for t in range(NT)]

        def use(j, last, key):
            if j is None:
                return FIRST.index(key)
            return j * len(STEP) + (len(FIRST) + (LAST if last else STEP).index(key))

        def bank(j, last, key):
            l = FIRST if j is None else LAST if last else STEP
            return gen_ps[l.index(key) % GENS]

        def splits(j, t):
            return t if j is None else j * (NT + 1) + (NT + 1 + t)

        T_AT = {9: 0, 11: 1, 13: 2, 15: 3}

        block = ctx.enter_context(nc.Block())

        @block.sync
        def _(sp):
            def load(j):
                sp.dma_start(xa[:, :, :], x1_dram[bass.ds(j, 1), :, :].rearrange("a (t p) d -> p (a t) d", p=P)).then_inc(x_loaded, 16)

            load(0)
            sp.dma_start(u1_raw[:, :, :], U1.rearrange("(k p) r -> p k r", p=P)).then_inc(w_loaded[0], 16)
            sp.dma_start(b2_row[:, :], b2.rearrange("(a n) -> a n", a=1)).then_inc(small_loaded, 16)
            sp.dma_start(b1c[:, :], b1.rearrange("(m p) -> p m", p=P), allow_slow_non_contiguous=True).then_inc(small_loaded, 16)
            sp.dma_start(v1_raw[:, :], V1).then_inc(w_loaded[1], 16)
            sp.dma_start(u2_raw[:, :, :], U2.rearrange("(m p) r -> p m r", p=P)).then_inc(w_loaded[2], 16)
            sp.dma_start(v2_raw[:, :], V2).then_inc(w_loaded[3], 16)

            def step(j, last):
                if not last:
                    sp.wait_ge(y_ready, j * NT + NT)
                    load(j + 1)
                for t in range(NT):
                    sp.wait_ge(evacuated, use(j, last, ("o", t)) + 1)
                    sp.dma_start(out[bass.ds(j, 1), t * P:(t + 1) * P, :].rearrange("a p d -> (a p) d"),
                                 y[:, t, :]).then_inc(stored, 16)

            with sp.Fori(0, B - 1) as j:
                step(j, False)
            step(B - 1, True)
            sp.wait_ge(stored, 16 * NT * B)

        @block.gpsimd
        def _(pool):
            pool.memset(ident[:, :], 0.0).then_inc(const_step, 1)
            pool.memset(ones_row[:, :], 1.0).then_inc(const_step, 1)
            pool.memset(minus_half[:, :], -0.5).then_inc(const_step, 1)
            pool.wait_ge(const_step, 3)
            pool.affine_select(out=ident[:, :], in_=ident[:, :], compare_op=ALU.not_equal, fill=1.0,
                               base=0, pattern=[[-1, P]], channel_multiplier=1).then_inc(const_made, 1)

            def rstds(done):
                wait_apart(pool, const_step, 3, mv_done, done * NT + NT)
                pool.tensor_scalar(varp[:, :], mv[:, :, 1], EPS, None, ALU.add).then_inc(var_done, 1)
                pool.wait_ge(var_done, done + 1)
                pool.tensor_tensor(rstd[:, :], varp[:, :], minus_half[:, :], ALU.pow).then_inc(rstd_done, 1)

            rstds(0)

            def step(j, last):
                pool.wait_ge(x_loaded, j * 16 + 16)
                pool.wait_ge(normed, j * NT + NT)
                pool.wait_ge(evacuated, 1)
                if not (isinstance(j, int) and j == 0):
                    pool.wait_ge(stored, j * (16 * NT))
                for t in range(NT):
                    pool.tensor_tensor(y[:, t, :], xa[:, t, :], b2_all[:, :], ALU.add).then_inc(y_ready, 1)
                if not last:
                    rstds(j + 1)

            step(0, False)
            with pool.Fori(1, B - 1) as j:
                step(j, False)
            step(B - 1, True)

        @block.scalar
        def _(act):
            def tile_hi(j, t):
                act.wait_ge(gen_ready, use(j, False, ("x", t)) + 1)
                nc.scalar.activation(xnT[:, 0, :, t * P:(t + 1) * P],
                                     bank(j, False, ("x", t))[:, :].rearrange("p (k t) -> p k t", k=NK), ACT.Copy).then_inc(rounded, 1)

            def p_hi(j):
                act.wait_ge(gen_ready, use(j, False, "p") + 1)
                nc.scalar.activation(pT[:, 0, :], bank(j, False, "p")[:, :], ACT.Copy).then_inc(rounded, 1)

            act.wait_ge(w_loaded[0], 16)
            nc.scalar.activation(u1[:, 0, :, :], u1_raw[:, :, :], ACT.Copy).then_inc(w_rounded, 1)
            for t in range(NT):
                tile_hi(None, t)
            act.wait_ge(w_loaded[1], 16)
            nc.scalar.activation(v1[:, 0, :], v1_raw[:, :], ACT.Copy).then_inc(w_rounded, 1)
            p_hi(None)
            act.wait_ge(w_loaded[2], 16)
            nc.scalar.activation(u2[:, 0, :, :], u2_raw[:, :, :], ACT.Copy).then_inc(w_rounded, 1)
            act.wait_ge(w_loaded[3], 16)
            nc.scalar.activation(v2[:, 0, :], v2_raw[:, :], ACT.Copy).then_inc(w_rounded, 1)
            act.wait_ge(small_loaded, 32)

            def step(j, last):
                tiles = j * NF
                for m in range(NF + 1):
                    if m < NF:
                        act.wait_ge(h_ready, tiles + m + 1)
                        if not (isinstance(j, int) and j == 0 and m < RING):
                            act.wait_ge(h_split, tiles + m + 1 - RING)
                        nc.scalar.activation(gelu[:, m % RING, :], h_ps[m % RING][:, :], ACT.Gelu_apprx_tanh,
                                             bias=b1c[:, m:m + 1]).then_inc(gelu_done, 1)
                    if m >= 1:
                        n = m - 1
                        act.wait_ge(gelu_done, tiles + n + 1)
                        if not (isinstance(j, int) and j == 0 and n < RING):
                            act.wait_ge(h_used, tiles + n + 1 - RING)
                        nc.scalar.activation(hT[:, n % RING, 0, :], gelu[:, n % RING, :], ACT.Copy).then_inc(h_rounded, 1)
                    if not last and m - 1 in T_AT:
                        tile_hi(j, T_AT[m - 1])
                act.wait_ge(h_used, tiles + NF)
                nc.scalar.activation(qT[:, 0, :], q_ps[:, :], ACT.Copy).then_inc(q_rounded, 1)
                if not last:
                    p_hi(j)

            step(0, False)
            with act.Fori(1, B - 1) as j:
                step(j, False)
            step(B - 1, True)

        @block.vector
        def _(dve):
            def minus(out, whole, hi_half):
                return nc.vector.tensor_tensor(out, whole, hi_half.bitcast(FP32), ALU.subtract)

            def tile_lo(j, t):
                dve.wait_ge(rounded, splits(j, t) + 1)
                cols = slice(t * P, (t + 1) * P)
                minus(xnT[:, 1, :, cols], bank(j, False, ("x", t))[:, :].rearrange("p (k t) -> p k t", k=NK),
                      xnT[:, 0, :, cols]).then_inc(evacuated, 1)

            def p_lo(j):
                dve.wait_ge(rounded, splits(j, NT) + 1)
                minus(pT[:, 1, :], bank(j, False, "p")[:, :], pT[:, 0, :]).then_inc(evacuated, 1)

            def norm_stats(done):
                dve.wait_ge(x_loaded, done * 16 + 16)
                for t in range(NT):
                    nc.vector.bn_stats(stats[:, t, :], xa[:, t, :]).then_inc(stats_done, 1)
                for t in range(NT):
                    wait_apart(dve, const_made, 1, stats_done, done * NT + t + 1)
                    nc.vector.bn_aggr(mv[:, t, :], stats[:, t, :]).then_inc(mv_done, 1)

            def normalise(done):
                dve.wait_ge(rstd_done, done + 1)
                for t in range(NT):
                    nc.vector.tensor_scalar(xn[:, t, :], xa[:, t, :], mv[:, t, 0:1], rstd[:, t:t + 1],
                                            ALU.subtract, ALU.mult).then_inc(normed, 1)

            dve.wait_ge(gen_ready, 1)
            nc.vector.tensor_copy(b2_all[:, :], bank(None, False, "b2")[:, :]).then_inc(evacuated, 1)
            norm_stats(0)
            dve.wait_ge(w_rounded, 1)
            minus(u1[:, 1, :, :], u1_raw[:, :, :], u1[:, 0, :, :]).then_inc(w_split, 1)
            normalise(0)
            for t in range(NT):
                tile_lo(None, t)
            dve.wait_ge(w_rounded, 2)
            minus(v1[:, 1, :], v1_raw[:, :], v1[:, 0, :]).then_inc(w_split, 1)
            p_lo(None)
            dve.wait_ge(w_rounded, 3)
            minus(u2[:, 1, :, :], u2_raw[:, :, :], u2[:, 0, :, :]).then_inc(w_split, 1)
            dve.wait_ge(w_rounded, 4)
            minus(v2[:, 1, :], v2_raw[:, :], v2[:, 0, :]).then_inc(w_split, 1)

            def step(j, last):
                tiles = j * NF
                for m in range(NF):
                    dve.wait_ge(h_rounded, tiles + m + 1)
                    minus(hT[:, m % RING, 1, :], gelu[:, m % RING, :], hT[:, m % RING, 0, :]).then_inc(h_split, 1)
                    if not last:
                        if m == 5:
                            norm_stats(j + 1)
                        if m == 7:
                            normalise(j + 1)
                        if m in T_AT:
                            tile_lo(j, T_AT[m])
                dve.wait_ge(q_rounded, j + 1)
                minus(qT[:, 1, :], q_ps[:, :], qT[:, 0, :]).then_inc(q_split, 1)
                if not last:
                    p_lo(j)
                for t in range(NT):
                    dve.wait_ge(gen_ready, use(j, last, ("o", t)) + 1)
                    dve.wait_ge(y_ready, j * NT + t + 1)
                    nc.vector.tensor_tensor(y[:, t, :], bank(j, last, ("o", t))[:, :], y[:, t, :], ALU.add).then_inc(evacuated, 1)

            step(0, False)
            with dve.Fori(1, B - 1) as j:
                step(j, False)
            step(B - 1, True)

        @block.tensor
        def _(pe):
            def claim(j, last, key):
                n = use(j, last, key)
                if j is not None or n >= GENS:
                    pe.wait_ge(evacuated, n - GENS + 1)
                return bank(j, last, key)

            def summed(ps, terms):
                for n, (left, right) in enumerate(terms):
                    done = nc.tensor.matmul(ps[:, :], left, right, start=(n == 0), stop=(n == len(terms) - 1))
                return done

            def tile(j, t, batch):
                ps = claim(j, False, ("x", t))
                pe.wait_ge(normed, batch * NT + (t + 1))
                for k in range(NK):
                    done = nc.tensor.transpose(ps[:, k * P:(k + 1) * P], xn[:, t, k * P:(k + 1) * P], ident[:, :])
                done.then_inc(gen_ready, 1)

            def first_product(j):
                ps = claim(j, False, "p")
                pe.wait_ge(evacuated, use(j, False, ("x", NT - 1)) + 1)
                summed(ps, [(u1[:, i, k, :], xnT[:, i2, k, :]) for k in range(NK) for i, i2 in TERMS]).then_inc(gen_ready, 1)

            pe.wait_ge(const_made, 1)
            pe.wait_ge(small_loaded, 32)
            nc.tensor.matmul(bank(None, False, "b2")[:, :], ones_row[:, :], b2_row[:, :], start=True, stop=True).then_inc(gen_ready, 1)
            for t in range(NT):
                tile(None, t, 0)
            pe.wait_ge(w_split, 1)
            first_product(None)
            pe.wait_ge(w_split, 4)

            def step(j, last):
                tiles = j * NF
                pe.wait_ge(evacuated, (use(None, False, "p") if isinstance(j, int) and j == 0 else use(j - 1, False, "p")) + 1)
                for m in range(NF + LAG):
                    if m < NF:
                        if not (isinstance(j, int) and j == 0 and m < RING):
                            pe.wait_ge(gelu_done, tiles + m + 1 - RING)
                        summed(h_ps[m % RING], [(v1[:, i, m * P:(m + 1) * P], pT[:, i2, :]) for i, i2 in TERMS]).then_inc(h_ready, 1)
                    if m >= LAG:
                        n = m - LAG
                        if n == 0 and not (isinstance(j, int) and j == 0):
                            pe.wait_ge(q_split, j)
                        pe.wait_ge(h_split, tiles + n + 1)
                        for i, (w, a) in enumerate(TERMS):
                            done = nc.tensor.matmul(q_ps[:, :], u2[:, w, n, :], hT[:, n % RING, a, :],
                                                    start=(n == 0 and i == 0), stop=(n == NF - 1 and i == 2))
                        done.then_inc(h_used, 1)
                    if not last and m in T_AT:
                        tile(j, T_AT[m], j + 1)
                if not last:
                    first_product(j)
                pe.wait_ge(q_split, j + 1)
                for t in range(NT):
                    ps = claim(j, last, ("o", t))
                    summed(ps, [(qT[:, i, t * P:(t + 1) * P], v2[:, i2, :]) for i, i2 in TERMS]).then_inc(gen_ready, 1)

            step(0, False)
            with pe.Fori(1, B - 1) as j:
                step(j, False)
            step(B - 1, True)


_INS = ["x", "ctx_1024", "L0_xattn_Wq", "L0_xattn_bq", "L0_xattn_Wk", "L0_xattn_bk", "L0_xattn_Wv", "L0_xattn_bv",
        "L0_xattn_Wo", "L0_xattn_bo", "L0_ffn_U1", "L0_ffn_V1", "L0_ffn_b1", "L0_ffn_U2", "L0_ffn_V2", "L0_ffn_b2"]


def build(nc, a, out):
    x1_dram = nc.dram_tensor("x1_scratch", (B, S, D), FP32).ap()
    attention_phase(nc, a["x"], a["ctx_1024"], *(a[f"L0_xattn_{n}"] for n in ("Wq", "bq", "Wk", "bk", "Wv", "bv", "Wo", "bo")), x1_dram)
    ffn_phase(nc, x1_dram, *(a[f"L0_ffn_{n}"] for n in ("U1", "V1", "b1", "U2", "V2", "b2")), out)


def kernel(**inputs):
    import numpy as _np
    import concourse.bacc as _bacc
    from concourse.bass_utils import run_bass_kernel_spmd as _run

    nc = _bacc.Bacc("TRN2", target_bir_lowering=False, num_devices=1)
    arrays, args = {}, {}
    for name in _INS:
        a = _np.ascontiguousarray(inputs[name])
        arrays[f"in_{name}_dram"] = a
        args[name] = nc.dram_tensor(f"in_{name}_dram", a.shape, mybir.dt.from_np(a.dtype), kind="ExternalInput").ap()
    out = nc.dram_tensor("out_0_dram", (B, S, D), FP32, kind="ExternalOutput").ap()
    build(nc, args, out)
    r = _run(nc, [arrays], core_ids=[0])
    return r.results[0]["out_0_dram"]
```

```python
import concourse.bass as bass
from concourse import mybir
from contextlib import ExitStack

FP32 = mybir.dt.float32
F32R = mybir.dt.float32r
BF16 = mybir.dt.bfloat16
ALU = mybir.AluOpType
ACT = mybir.ActivationFunctionType
AXIS_X = mybir.AxisListType.X

B, S, D = 8, 512, 512
P = 128
H, HD = 16, 32
NT = S // P
NK = D // P
HG = P // HD
NG = H // HG
FF, R = 2048, 128
NF = FF // P
EPS = 1e-5
SCALE = 1.0 / (HD ** 0.5)
MASKED = -3.0e38
UNITS = 10
A_UNITS, B_UNITS = HG, HG

TERMS = ((0, 0), (0, 1), (1, 0))


def wait_apart(eng, met, count, sem, value):
    if not isinstance(value, int):
        value = eng.to_reg(value)
    eng.wait_ge(met, count)
    eng.wait_ge(sem, value)


def attention_phase(nc, x, ctx_in, Wq, bq, Wk, bk, Wv, bv, Wo, bo, x1_dram):
    with ExitStack() as ctx:
        def sb(name, shape, dt=FP32):
            return ctx.enter_context(nc.sbuf_tensor(name, shape, dt))

        def sem(name):
            return ctx.enter_context(nc.semaphore(name))

        wqT = sb("wqT", [P, 2, NK, D], F32R)
        wkT = sb("wkT", [P, 2, NK, D], F32R)
        wvT = sb("wvT", [P, 2, NK, D], F32R)
        woT = sb("woT", [P, 2, NK, D], F32R)
        xnT = sb("xnT", [P, 2, NK, S], F32R)
        cxT = sb("cxT", [P, 2, NK, S], F32R)
        attnT = sb("attnT", [P, 2, NK, S], F32R)
        QLO, QHI, KHI, KLO = range(4)
        qk = sb("qk", [P, 4, S], F32R)
        M_ROW = 3 * HD
        qs = sb("qs", [P, 2, 2, HG, S], F32R)
        v = sb("v", [P, NT, D])
        probs = sb("probs", [P, UNITS, S])
        xbuf = sb("xbuf", [P, NT, D])
        cbuf = sb("cbuf", [P, NT, D])
        attn = sb("attn", [P, S])
        max_split = sb("max_split", [P, NT, 2, HG])
        mrow = sb("mrow", [2 * HG, S], F32R)
        negmax = sb("negmax", [P, NT, HG])
        bo_all = sb("bo_all", [P, D])
        ident = sb("ident", [P, P])
        ident16 = sb("ident16", [P, P], BF16)
        mask16 = sb("mask16", [P, P], BF16)
        ones32 = sb("ones32", [P, HD])
        ones_row = sb("ones_row", [1, P])
        bqc = sb("bqc", [P, NK])
        bkc = sb("bkc", [P, NK])
        bvc = sb("bvc", [P, NK])
        stats = sb("stats", [P, NT, 6])
        mv = sb("mv", [P, NT, 2])
        rstd = sb("rstd", [P, NT])
        varp = sb("varp", [P, NT])
        minus_half = sb("minus_half", [P, NT])

        psum = [ctx.enter_context(nc.psum_tensor(f"ps{i}", [P, 512], FP32)) for i in range(8)]
        score_ps, max_ps, gen_ps, out_ps, den_ps = psum[0:2], psum[2:4], psum[4:6], psum[6], psum[7]

        w_loaded = [sem(f"w_loaded{i}") for i in range(4)]
        small_loaded = sem("small_loaded")
        bo_loaded = sem("bo_loaded")
        ident_made = sem("ident_made")
        const_step = sem("const_step")
        stack_made = sem("stack_made")
        w_ready = sem("w_ready")
        w_rounded = sem("w_rounded")
        w_split = sem("w_split")
        max_hi = sem("max_hi")
        max_lo = sem("max_lo")
        x_loaded = sem("x_loaded")
        ctx_loaded = sem("ctx_loaded")
        gen_ready = sem("gen_ready")
        rounded = sem("rounded")
        evacuated = sem("evacuated")
        stacked = sem("stacked")
        m_stacked = sem("m_stacked")
        max_ready = sem("max_ready")
        max_done = sem("max_done")
        score_ready = sem("score_ready")
        exp_done = sem("exp_done")
        masked = sem("masked")
        folded = sem("folded")
        av0_done = sem("av0_done")
        av_done = sem("av_done")
        recip_done = sem("recip_done")
        attn_scaled = sem("attn_scaled")
        attn_rounded = sem("attn_rounded")
        attn_ready = sem("attn_ready")
        stats_done = sem("stats_done")
        mv_done = sem("mv_done")
        var_done = sem("var_done")
        rstd_done = sem("rstd_done")
        normed = sem("normed")
        residual_ready = sem("residual_ready")
        x1_stored = sem("x1_stored")

        TOKENS = [("c", t) for t in range(NT)] + [("x", t) for t in range(NT)]
        VALUES = [("v", t) for t in range(NT)]
        OUTS = [("o", t) for t in range(NT)]
        AHEAD = [("bo",)] + TOKENS + [("q", -2), ("k", -2), ("q", -1), ("k", -1)] + VALUES + [("m", -1)]

        def in_step(kind):
            uses = []
            for g in range(NG):
                if projects(kind, g):
                    uses += [("q", g), ("k", g)]
                if looks_ahead(kind, g):
                    uses.append(("m", g))
                if g == 0 and kind != "first":
                    uses += OUTS
                if g == 1 and kind != "last":
                    uses += TOKENS
                if g == NG - 1 and kind != "last":
                    uses += VALUES
            return uses

        def projects(kind, g):
            return not (kind == "last" and g >= 2)

        def looks_ahead(kind, g):
            return not (kind == "last" and g == NG - 1)

        def uses_of(kind):
            return {"ahead": AHEAD, "tail": OUTS}.get(kind) or in_step(kind)

        def before(b, kind, width):
            if kind == "ahead":
                return 0
            if kind == "first":
                return width(AHEAD)
            sofar = width(AHEAD) + width(in_step("first"))
            if kind == "tail":
                return sofar + (B - 2) * width(in_step("mid")) + width(in_step("last"))
            return b * width(in_step("mid")) + (sofar - width(in_step("mid")))

        SPLIT = "cxqk"

        def splits(l):
            return sum(u[0] in SPLIT for u in l)

        def use(b, kind, key):
            return before(b, kind, len) + uses_of(kind).index(key)

        def split(b, kind, key):
            l = uses_of(kind)
            return before(b, kind, splits) + splits(l[:l.index(key)])

        def bank(kind, key):
            return gen_ps[uses_of(kind).index(key) % 2]

        for kind in ("ahead", "first", "mid"):
            assert len(uses_of(kind)) % 2 == 0

        def steps(eng, step):
            step(0, "first")
            with eng.Fori(1, B - 1) as b:
                step(b, "mid")
            step(B - 1, "last")

        def unit(u):
            if u < A_UNITS:
                return "A", u
            if u < A_UNITS + B_UNITS:
                return "B", u - A_UNITS
            return "C", u - A_UNITS - B_UNITS

        K_LO, K_MID, K_HI = P, 2 * P, 3 * P
        GROUP = NG * UNITS
        STACK_DMAS = 3 * HG
        weight_ps = score_ps + max_ps + [out_ps, den_ps]
        WEIGHTS = ((wqT, probs[:, 0:NK, :]), (wkT, probs[:, NK:2 * NK, :]), (wvT, v[:, :, :]), (woT, probs[:, 0:NK, :]))

        block = ctx.enter_context(nc.Block())

        @block.sync
        def _(sp):
            def load_weight(i, w):
                sp.dma_start(WEIGHTS[i][1], w.rearrange("(m p) n -> p m n", p=P)).then_inc(w_loaded[i], 16)

            def load_tokens(to, of, b, loaded):
                sp.dma_start(to[:, :, :], of[bass.ds(b, 1), :, :].rearrange("a (t p) d -> p (a t) d", p=P)).then_inc(loaded, 16)

            def stack(slot):
                for h in range(HG):
                    rows = slice(h * HD, (h + 1) * HD)
                    for row, pair in enumerate((slice(QHI, KHI + 1), slice(QLO, KHI + 1, 2), slice(QHI, KLO + 1, 2))):
                        sp.dma_start(qs[row * HD:(row + 1) * HD, slot, :, h, :].bitcast(FP32),
                                     qk[rows, pair, :].bitcast(FP32)).then_inc(stacked, 16)

            def stack_max(slot):
                for half in range(2):
                    sp.dma_start(qs[M_ROW + half:M_ROW + half + 1, slot, 0, :, :].bitcast(FP32),
                                 mrow[half * HG:(half + 1) * HG, :].bitcast(FP32)).then_inc(m_stacked, 16)

            def store_x1(b, at, kind):
                for t in range(NT):
                    sp.wait_ge(evacuated, use(at, kind, ("o", t)) + 1)
                    sp.dma_start(x1_dram[bass.ds(b, 1), t * P:(t + 1) * P, :].rearrange("a p d -> (a p) d"),
                                 xbuf[:, t, :]).then_inc(x1_stored, 16)

            load_weight(0, Wq)
            load_tokens(xbuf, x, 0, x_loaded)
            load_tokens(cbuf, ctx_in, 0, ctx_loaded)
            load_weight(1, Wk)
            load_weight(2, Wv)
            for b_, c in ((bq, bqc), (bk, bkc), (bv, bvc)):
                sp.dma_start(c[:, :], b_.rearrange("(m p) -> p m", p=P), allow_slow_non_contiguous=True).then_inc(small_loaded, 16)
            sp.dma_start(attn[0:1, :], bo.rearrange("(a n) -> a n", a=1)).then_inc(bo_loaded, 16)
            sp.wait_ge(w_ready, NK)
            load_weight(3, Wo)
            sp.wait_ge(stack_made, 4)
            for n in (0, 1):
                sp.wait_ge(evacuated, use(None, "ahead", ("k", n - 2)) + 1)
                stack(n)
            sp.wait_ge(evacuated, use(None, "ahead", ("m", -1)) + 1)
            stack_max(0)

            def step(b, kind):
                if kind == "first":
                    sp.wait_ge(gen_ready, use(None, "ahead", ("x", NT - 1)) + 1)
                    load_tokens(xbuf, x, b + 1, x_loaded)
                if kind != "last":
                    load_tokens(cbuf, ctx_in, b + 1, ctx_loaded)
                for g in range(NG):
                    if looks_ahead(kind, g):
                        sp.wait_ge(evacuated, use(b, kind, ("m", g)) + 1)
                        stack_max((g + 1) % 2)
                    if projects(kind, g):
                        wait_apart(sp, stack_made, 4, evacuated, use(b, kind, ("k", g)) + 1)
                        sp.wait_ge(score_ready, b * GROUP + UNITS * (g + 1))
                        stack(g % 2)
                    if g == 0 and kind != "first":
                        store_x1(b - 1, b, kind)
                        sp.wait_ge(x1_stored, b * (16 * NT))
                        load_tokens(xbuf, x, (b + 1) if kind == "mid" else b, x_loaded)
                    if g == 1 and kind != "last":
                        sp.wait_ge(gen_ready, use(b, kind, ("x", NT - 1)) + 1)
                        load_tokens(xbuf, x, b, x_loaded)

            steps(sp, step)
            store_x1(B - 1, None, "tail")
            sp.wait_ge(x1_stored, 16 * NT * B)

        @block.gpsimd
        def _(pool):
            pool.memset(ident[:, :], 0.0).then_inc(const_step, 1)
            pool.wait_ge(const_step, 1)
            pool.affine_select(out=ident[:, :], in_=ident[:, :], compare_op=ALU.not_equal, fill=1.0,
                               base=0, pattern=[[-1, P]], channel_multiplier=1).then_inc(ident_made, 1)
            pool.memset(minus_half[:, :], -0.5).then_inc(const_step, 1)
            pool.memset(mask16[:, :], 0.0).then_inc(const_step, 1)
            pool.memset(ones32[:, :], 1.0).then_inc(const_step, 1)
            pool.memset(ones_row[:, :], 1.0).then_inc(const_step, 1)
            pool.wait_ge(const_step, 5)
            pool.affine_select(out=mask16[:, :], in_=mask16[:, :], compare_op=ALU.is_ge, fill=MASKED,
                               base=0, pattern=[[-1, P]], channel_multiplier=1).then_inc(const_step, 1)
            pool.wait_ge(ident_made, 1)
            pool.tensor_copy(ident16[:, :], ident[:, :]).then_inc(const_step, 1)

            def rstds(done):
                wait_apart(pool, const_step, 2, mv_done, done * NT + NT)
                pool.tensor_scalar(varp[:, :], mv[:, :, 1], EPS, None, ALU.add).then_inc(var_done, 1)
                pool.wait_ge(var_done, done + 1)
                pool.tensor_tensor(rstd[:, :], varp[:, :], minus_half[:, :], ALU.pow).then_inc(rstd_done, 1)

            pool.wait_ge(const_step, 7)
            for slot in range(2):
                pool.memset(qs[M_ROW:P, slot, :, :, :].bitcast(FP32), 0.0).then_inc(stack_made, 1)
            pool.wait_ge(stack_made, 2)
            for slot in range(2):
                pool.memset(qs[M_ROW:M_ROW + 2, slot, 1, :, :].bitcast(FP32), 1.0).then_inc(stack_made, 1)
            pool.wait_ge(stack_made, 4)
            rstds(0)

            def causal(view):
                pool.affine_select(out=view, in_=view, compare_op=ALU.is_ge, fill=0.0, base=0,
                                   pattern=[[0, HG], [1, P]], channel_multiplier=-1).then_inc(masked, 1)

            pa, pb, pc = probs[:, 0:HG, :], probs[:, HG:2 * HG, :], probs[:, 2 * HG:UNITS, :]
            pc4 = pc.rearrange("p c (h q) -> p (c h) q", h=2)

            def step(b, kind):
                for g in range(NG):
                    grp = b * NG + g
                    units = b * GROUP + g * UNITS
                    wait_apart(pool, const_step, 7, exp_done, units + A_UNITS)
                    causal(pa[:, :, 0:P])
                    wait_apart(pool, const_step, 7, exp_done, units + A_UNITS + B_UNITS)
                    causal(pb[:, :, 0:P])
                    causal(pb[:, :, K_HI:S])
                    wait_apart(pool, const_step, 7, exp_done, units + UNITS)
                    causal(pc4[:, :, 0:P])
                    pool.wait_ge(av0_done, grp + 1)
                    pool.wait_ge(masked, grp * 4 + 4)
                    pool.tensor_tensor(pa[:, :, K_LO:S], pa[:, :, K_LO:S], pb[:, :, 0:S - K_LO], ALU.add).then_inc(folded, 1)
                    pool.wait_ge(folded, grp * 3 + 1)
                    pool.tensor_tensor(pa[:, :, K_MID:S], pa[:, :, K_MID:S], pc4, ALU.add).then_inc(folded, 1)
                    pool.wait_ge(folded, grp * 3 + 2)
                    pool.tensor_tensor(pa[:, :, K_HI:S], pa[:, :, K_HI:S], pb[:, :, K_HI:S], ALU.add).then_inc(folded, 1)
                    if g == 1 and kind != "last":
                        rstds(b + 1)
                    if g >= 2:
                        pool.wait_ge(x_loaded, b * 32 + (32 if kind == "last" else 48))
                        pool.wait_ge(evacuated, use(None, "ahead", ("bo",)) + 1)
                        for t in range((g - 2) * 2, (g - 1) * 2):
                            pool.tensor_tensor(xbuf[:, t, :], xbuf[:, t, :], bo_all[:, :], ALU.add).then_inc(residual_ready, 1)

            steps(pool, step)

        @block.scalar
        def _(act):
            def gen(kind, key):
                ps = bank(kind, key)
                return ps[:, :].rearrange("p (k t) -> p k t", k=NK) if key[0] in "cx" else ps[:, :]

            def hi(out, b, kind, key, bias=None):
                act.wait_ge(gen_ready, use(b, kind, key) + 1)
                if bias is None:
                    nc.scalar.activation(out, gen(kind, key), ACT.Copy).then_inc(rounded, 1)
                else:
                    nc.scalar.activation(out, gen(kind, key), ACT.Identity, bias=bias).then_inc(rounded, 1)

            def weight_hi(i):
                for k in range(NK):
                    n = i * NK + k
                    act.wait_ge(w_ready, n + 1)
                    nc.scalar.activation(WEIGHTS[i][0][:, 0, k, :], weight_ps[n % 6][:, :], ACT.Copy).then_inc(w_rounded, 1)

            def tokens_hi(b, kind):
                for name, to in (("c", cxT), ("x", xnT)):
                    for t in range(NT):
                        hi(to[:, 0, :, t * P:(t + 1) * P], b, kind, (name, t))

            def attn_hi(grp, g):
                act.wait_ge(attn_scaled, grp + 1)
                nc.scalar.activation(attnT[:, 0, g, :], attn[:, :], ACT.Identity, bias=bvc[:, g:g + 1]).then_inc(attn_rounded, 1)

            weight_hi(0)
            tokens_hi(None, "ahead")
            weight_hi(1)
            act.wait_ge(small_loaded, 48)
            for g in (-2, -1):
                if g == -1:
                    act.wait_ge(stacked, 16 * STACK_DMAS)
                hi(qk[:, QHI, :], None, "ahead", ("q", g), bqc[:, g + 2:g + 3])
                hi(qk[:, KHI, :], None, "ahead", ("k", g), bkc[:, g + 2:g + 3])
                weight_hi(g + 4)

            def step(b, kind):
                for g in range(NG):
                    grp = b * NG + g
                    units = b * GROUP + g * UNITS
                    mt = (g + 2) % NG
                    for u in range(UNITS):
                        act.wait_ge(score_ready, units + u + 1)
                        nc.scalar.activation(probs[:, u, :], score_ps[u % 2][:, :], ACT.Exp, scale=SCALE).then_inc(exp_done, 1)
                        if u == 8 and not (kind == "first" and g == 0):
                            attn_hi(grp - 1, (g - 1) % NG)
                    if projects(kind, g):
                        act.wait_ge(stacked, (grp + 2) * (16 * STACK_DMAS))
                        hi(qk[:, QHI, :], b, kind, ("q", g), bqc[:, mt:mt + 1])
                        hi(qk[:, KHI, :], b, kind, ("k", g), bkc[:, mt:mt + 1])
                    if g == 1 and kind != "last":
                        tokens_hi(b, kind)

            steps(act, step)
            attn_hi(B * NG - 1, NG - 1)

        @block.vector
        def _(dve):
            def gen(kind, key):
                ps = bank(kind, key)
                return ps[:, :].rearrange("p (k t) -> p k t", k=NK) if key[0] in "cx" else ps[:, :]

            def lo(out, hi_half, b, kind, key, bias=None):
                dve.wait_ge(rounded, split(b, kind, key) + 1)
                hi_half = hi_half.bitcast(FP32)
                if bias is None:
                    nc.vector.tensor_tensor(out, gen(kind, key), hi_half, ALU.subtract).then_inc(evacuated, 1)
                else:
                    nc.vector.scalar_tensor_tensor(out, gen(kind, key), bias, hi_half, ALU.add, ALU.subtract).then_inc(evacuated, 1)

            def weight_lo(i):
                for k in range(NK):
                    n = i * NK + k
                    dve.wait_ge(w_rounded, n + 1)
                    nc.vector.tensor_tensor(WEIGHTS[i][0][:, 1, k, :], weight_ps[n % 6][:, :],
                                            WEIGHTS[i][0][:, 0, k, :].bitcast(FP32), ALU.subtract).then_inc(w_split, 1)

            def tile_stats(t):
                nc.vector.bn_stats(stats[:, t, :], xbuf[:, t, :]).then_inc(stats_done, 1)

            def mean_and_variance(done):
                for t in range(NT):
                    wait_apart(dve, ident_made, 1, stats_done, done * NT + t + 1)
                    nc.vector.bn_aggr(mv[:, t, :], stats[:, t, :]).then_inc(mv_done, 1)

            def normalise(done):
                dve.wait_ge(rstd_done, done + 1)
                for t in range(NT):
                    nc.vector.tensor_scalar(xbuf[:, t, :], xbuf[:, t, :], mv[:, t, 0:1], rstd[:, t:t + 1],
                                            ALU.subtract, ALU.mult).then_inc(normed, 1)

            def tokens_lo(b, kind, name, to):
                for t in range(NT):
                    cols = slice(t * P, (t + 1) * P)
                    lo(to[:, 1, :, cols], to[:, 0, :, cols], b, kind, (name, t))

            def maxima(n_units, u):
                dve.wait_ge(max_ready, n_units + u + 1)
                kind, j = unit(u)
                ps = max_ps[u % 2]

                def take(out, in_):
                    return nc.vector.tensor_reduce(out, in_, AXIS_X, ALU.max, negate=True)

                if kind == "A":
                    take(negmax[:, 3, j:j + 1], ps[:, :]).then_inc(max_done, 1)
                elif kind == "B":
                    take(negmax[:, 0, j:j + 1], ps[:, 0:P])
                    take(negmax[:, 2, j:j + 1], ps[:, P:S]).then_inc(max_done, 1)
                else:
                    take(negmax[:, 1, 2 * j:2 * j + 2], ps[:, :].rearrange("p (h k) -> p h k", h=2)).then_inc(max_done, 1)

            def split_maxima(n):
                dve.wait_ge(max_done, n * UNITS + UNITS)
                nc.vector.tensor_copy(max_split[:, :, 0, :].bitcast(F32R), negmax[:, :, :]).then_inc(max_hi, 1)
                dve.wait_ge(max_hi, n + 1)
                nc.vector.tensor_tensor(max_split[:, :, 1, :], negmax[:, :, :], max_split[:, :, 0, :],
                                        ALU.subtract).then_inc(max_lo, 1)

            def maxima_out(b, kind, g):
                dve.wait_ge(gen_ready, use(b, kind, ("m", g)) + 1)
                nc.vector.tensor_copy(mrow[:, :], bank(kind, ("m", g))[0:2 * HG, :]).then_inc(evacuated, 1)

            def attn_scale(b, kind, grp):
                if kind != "first" or grp:
                    if not (isinstance(grp, int) and grp == 0):
                        dve.wait_ge(attn_ready, grp)
                dve.wait_ge(av_done, grp + 1)
                nc.vector.reciprocal(attn[:, :], den_ps[:, :]).then_inc(recip_done, 1)
                dve.wait_ge(recip_done, grp + 1)
                nc.vector.tensor_tensor(attn[:, :], out_ps[:, :], attn[:, :], ALU.mult).then_inc(attn_scaled, 1)

            def attn_lo(grp, g):
                dve.wait_ge(attn_rounded, grp + 1)
                nc.vector.scalar_tensor_tensor(attnT[:, 1, g, :], attn[:, :], bvc[:, g:g + 1],
                                               attnT[:, 0, g, :].bitcast(FP32), ALU.add, ALU.subtract).then_inc(attn_ready, 1)

            def values(b, kind):
                for t in range(NT):
                    dve.wait_ge(gen_ready, use(b, kind, ("v", t)) + 1)
                    nc.vector.tensor_copy(v[:, t, :], bank(kind, ("v", t))[:, :]).then_inc(evacuated, 1)

            def outs(b, at, kind):
                for t in range(NT):
                    dve.wait_ge(gen_ready, use(at, kind, ("o", t)) + 1)
                    dve.wait_ge(residual_ready, b * NT + t + 1)
                    nc.vector.tensor_tensor(xbuf[:, t, :], bank(kind, ("o", t))[:, :], xbuf[:, t, :], ALU.add).then_inc(evacuated, 1)

            dve.wait_ge(x_loaded, 16)
            for t in range(NT):
                tile_stats(t)
            mean_and_variance(0)
            weight_lo(0)
            dve.wait_ge(gen_ready, use(None, "ahead", ("bo",)) + 1)
            nc.vector.tensor_copy(bo_all[:, :], bank("ahead", ("bo",))[:, :]).then_inc(evacuated, 1)
            normalise(0)
            tokens_lo(None, "ahead", "c", cxT)
            tokens_lo(None, "ahead", "x", xnT)
            weight_lo(1)
            dve.wait_ge(small_loaded, 48)
            for g in (-2, -1):
                lo(qk[:, QLO, :], qk[:, QHI, :], None, "ahead", ("q", g), bqc[:, g + 2:g + 3])
                lo(qk[:, KLO, :], qk[:, KHI, :], None, "ahead", ("k", g), bkc[:, g + 2:g + 3])
                weight_lo(g + 4)
            values(None, "ahead")
            for u in range(UNITS):
                maxima(0, u)
            split_maxima(0)
            maxima_out(None, "ahead", -1)

            def step(b, kind):
                for g in range(NG):
                    grp = b * NG + g
                    mt = (g + 2) % NG
                    if not (kind == "first" and g == 0):
                        attn_scale(b, kind, grp - 1)
                        attn_lo(grp - 1, (g - 1) % NG)
                    if projects(kind, g):
                        lo(qk[:, QLO, :], qk[:, QHI, :], b, kind, ("q", g), bqc[:, mt:mt + 1])
                    if looks_ahead(kind, g):
                        for u in range(UNITS):
                            maxima(b * GROUP + (g + 1) * UNITS, u)
                            if g == 1 and kind != "last" and u % 2 and u < 2 * NT:
                                if u == 1:
                                    dve.wait_ge(x_loaded, b * 32 + 32)
                                tile_stats(u // 2)
                        split_maxima(grp + 1)
                        if g == 1 and kind != "last":
                            mean_and_variance(b + 1)
                    if projects(kind, g):
                        lo(qk[:, KLO, :], qk[:, KHI, :], b, kind, ("k", g), bkc[:, mt:mt + 1])
                    if looks_ahead(kind, g):
                        maxima_out(b, kind, g)
                    if g == 0 and kind != "first":
                        outs(b - 1, b, kind)
                    if g == 1 and kind != "last":
                        tokens_lo(b, kind, "c", cxT)
                        normalise(b + 1)
                        tokens_lo(b, kind, "x", xnT)
                    if g == NG - 1 and kind != "last":
                        values(b, kind)

            steps(dve, step)
            attn_scale(None, "tail", B * NG - 1)
            attn_lo(B * NG - 1, NG - 1)
            outs(B - 1, None, "tail")

        @block.tensor
        def _(pe):
            def claim(b, kind, key):
                n = use(b, kind, key)
                if kind != "ahead" or n >= 2:
                    pe.wait_ge(evacuated, n - 1)
                return bank(kind, key)

            def transposed(ps, of):
                for k in range(4):
                    done = nc.tensor.transpose(ps[:, k * P:(k + 1) * P], of(k), ident[:, :])
                return done

            def product(ps, left, right):
                todo = [(k, i, j) for k in range(NK) for i, j in TERMS]

                def issue(n):
                    k, i, j = todo[n]
                    return nc.tensor.matmul(ps[:, :], left(i, k), right(j, k), start=(n == 0), stop=(n == len(todo) - 1))
                return len(todo), issue

            def q_product(ps, mt):
                return product(ps, lambda i, k: wqT[:, i, k, mt * P:(mt + 1) * P], lambda j, k: xnT[:, j, k, :])

            def k_product(ps, mt):
                return product(ps, lambda i, k: wkT[:, i, k, mt * P:(mt + 1) * P], lambda j, k: cxT[:, j, k, :])

            def whole(made):
                n, issue = made
                for i in range(n):
                    done = issue(i)
                done.then_inc(gen_ready, 1)

            def weight(i):
                pe.wait_ge(w_loaded[i], 16)
                for k in range(NK):
                    n = i * NK + k
                    if n >= 6:
                        pe.wait_ge(w_split, n - 5)
                    transposed(weight_ps[n % 6], lambda m: WEIGHTS[i][1][:, m, k * P:(k + 1) * P]).then_inc(w_ready, 1)

            def tokens(b, kind):
                nxt = 0 if kind == "ahead" else b + 1
                pe.wait_ge(ctx_loaded, nxt * 16 + 16)
                for t in range(NT):
                    ps = claim(b, kind, ("c", t))
                    transposed(ps, lambda k: cbuf[:, t, k * P:(k + 1) * P]).then_inc(gen_ready, 1)
                for t in range(NT):
                    ps = claim(b, kind, ("x", t))
                    pe.wait_ge(normed, nxt * NT + (t + 1))
                    transposed(ps, lambda k: xbuf[:, t, k * P:(k + 1) * P]).then_inc(gen_ready, 1)

            def values(b, kind):
                for t in range(NT):
                    whole(product(claim(b, kind, ("v", t)), lambda i, k: cxT[:, i, k, t * P:(t + 1) * P],
                                  lambda j, k: wvT[:, j, k, :]))

            def outs(b, kind):
                for t in range(NT):
                    whole(product(claim(b, kind, ("o", t)), lambda i, k: attnT[:, i, k, t * P:(t + 1) * P],
                                  lambda j, k: woT[:, j, k, :]))

            def max_unit(units, slot, u):
                if not (isinstance(units, int) and units + u < 2):
                    pe.wait_ge(max_done, units + u - 1)
                kind, j = unit(u)
                ps = max_ps[u % 2]

                def scores(h, qt, c0, c1):
                    nc.tensor.matmul(ps[:, c0:c1], qs[0:M_ROW, slot, 0, h, qt * P:(qt + 1) * P],
                                     qs[0:M_ROW, slot, 1, h, 0:c1 - c0], start=True, stop=False)

                def mask(c):
                    return nc.tensor.matmul(ps[:, c:c + P], ident16[:, :], mask16[:, :], start=False, stop=True)

                if kind == "A":
                    scores(j, 3, 0, S)
                    done = mask(3 * P)
                elif kind == "B":
                    scores(j, 0, 0, 2 * P)
                    mask(0)
                    scores(j, 2, P, S)
                    done = mask(3 * P)
                else:
                    for i in range(2):
                        scores(2 * j + i, 1, i * 2 * P, (i + 1) * 2 * P)
                        done = mask((2 * i + 1) * P)
                done.then_inc(max_ready, 1)

            def score_unit(units, slot, u):
                if not (isinstance(units, int) and units + u < 2):
                    pe.wait_ge(exp_done, units + u - 1)
                kind, j = unit(u)
                ps = score_ps[u % 2]

                def scores(h, kt, q0, c0, c1):
                    return nc.tensor.matmul(ps[:, c0:c1], qs[:, slot, 1, h, kt * P:(kt + 1) * P],
                                            qs[:, slot, 0, h, q0:q0 + c1 - c0], start=True, stop=True)

                if kind == "A":
                    done = scores(j, 0, 0, 0, S)
                elif kind == "B":
                    scores(j, 3, 2 * P, 2 * P, S)
                    done = scores(j, 1, P, 0, 3 * P)
                else:
                    scores(2 * j, 2, 2 * P, 0, 2 * P)
                    done = scores(2 * j + 1, 2, 2 * P, 2 * P, S)
                done.then_inc(score_ready, 1)

            def maxima_across(b, kind, g, n):
                ps = claim(b, kind, ("m", g))
                pe.wait_ge(max_lo, n + 1)
                for t in range(NT):
                    done = nc.tensor.transpose(ps[0:2 * HG, t * P:(t + 1) * P],
                                               max_split[:, t, :, :].rearrange("p s h -> p (s h)"), ident[:, :])
                done.then_inc(gen_ready, 1)

            def weigh(g, kt, of):
                for h in range(HG):
                    done = nc.tensor.matmul(out_ps[h * HD:(h + 1) * HD, kt * P:S],
                                            v[:, kt, g * P + h * HD:g * P + (h + 1) * HD], of(h),
                                            start=(kt == 0), stop=(kt == 2))
                return done

            pe.wait_ge(ident_made, 1)
            weight(0)
            pe.wait_ge(bo_loaded, 16)
            pe.wait_ge(const_step, 7)
            nc.tensor.matmul(claim(None, "ahead", ("bo",))[:, :], ones_row[:, :], attn[0:1, :],
                             start=True, stop=True).then_inc(gen_ready, 1)
            tokens(None, "ahead")
            weight(1)
            pe.wait_ge(w_split, NK)
            pe.wait_ge(evacuated, use(None, "ahead", ("x", NT - 1)) + 1)
            for g in (-2, -1):
                whole(q_product(claim(None, "ahead", ("q", g)), g + 2))
                pe.wait_ge(w_split, 2 * NK)
                whole(k_product(claim(None, "ahead", ("k", g)), g + 2))
                weight(g + 4)
            pe.wait_ge(w_split, 4 * NK)
            values(None, "ahead")
            pe.wait_ge(stacked, 16 * STACK_DMAS)
            for u in range(UNITS):
                max_unit(0, 0, u)
            maxima_across(None, "ahead", -1, 0)

            pa, pb, pc = probs[:, 0:HG, :], probs[:, HG:2 * HG, :], probs[:, 2 * HG:UNITS, :]

            def step(b, kind):
                for g in range(NG):
                    grp = b * NG + g
                    units = b * GROUP + g * UNITS
                    mt = (g + 2) % NG

                    pe.wait_ge(m_stacked, grp * 32 + 32)
                    issued = 0
                    for u in range(UNITS):
                        score_unit(units, g % 2, u)
                        if projects(kind, g) and u >= 1:
                            if u == 1:
                                if g == 2:
                                    pe.wait_ge(evacuated, use(b, kind, ("x", NT - 1)) + 1)
                                nq, issue = q_product(claim(b, kind, ("q", g)), mt)
                            until = u * nq // (UNITS - 1)
                            for i in range(issued, until):
                                done = issue(i)
                            issued = until
                    if projects(kind, g):
                        done.then_inc(gen_ready, 1)

                    pe.wait_ge(masked, grp * 4 + 1)
                    if kind == "first":
                        if g == 0:
                            pe.wait_ge(evacuated, use(None, "ahead", ("v", NT - 1)) + 1)
                        else:
                            pe.wait_ge(attn_scaled, grp)
                    else:
                        if g == 0:
                            pe.wait_ge(evacuated, use(b, kind, ("q", 0)))
                        pe.wait_ge(attn_scaled, grp)
                    weigh(g, 0, lambda h: pa[:, h, :]).then_inc(av0_done, 1)

                    if projects(kind, g):
                        nk, issue = k_product(claim(b, kind, ("k", g)), mt)
                    if looks_ahead(kind, g):
                        pe.wait_ge(stacked, (grp + 2) * (16 * STACK_DMAS))
                    issued = 0
                    for u in range(UNITS):
                        if looks_ahead(kind, g):
                            max_unit(units + UNITS, (g + 1) % 2, u)
                        if projects(kind, g):
                            until = min(nk, (u + 1) * nk // (UNITS - 1))
                            for i in range(issued, until):
                                done = issue(i)
                                if i == nk - 1:
                                    done.then_inc(gen_ready, 1)
                            issued = until

                    pe.wait_ge(masked, grp * 4 + 3)
                    weigh(g, 1, lambda h: pb[:, h, 0:S - K_LO])
                    if looks_ahead(kind, g):
                        maxima_across(b, kind, g, grp + 1)
                    weigh(g, 3, lambda h: pb[:, h, K_HI:S])
                    pe.wait_ge(masked, grp * 4 + 4)
                    weigh(g, 2, lambda h: pc[:, h // 2, (h % 2) * K_MID:(h % 2 + 1) * K_MID])
                    pe.wait_ge(folded, grp * 3 + 3)
                    for h in range(HG):
                        done = nc.tensor.matmul(den_ps[h * HD:(h + 1) * HD, :], ones32[:, :], pa[:, h, :], start=True, stop=True)
                    done.then_inc(av_done, 1)

                    if g == 0 and kind != "first":
                        pe.wait_ge(attn_ready, b * NG)
                        outs(b, kind)
                    if g == 1 and kind != "last":
                        tokens(b, kind)
                    if g == NG - 1 and kind != "last":
                        values(b, kind)

            steps(pe, step)
            pe.wait_ge(attn_ready, B * NG)
            outs(None, "tail")


def ffn_phase(nc, x1_dram, U1, V1, b1, U2, V2, b2, out):
    with ExitStack() as ctx:
        def sb(name, shape, dt=FP32):
            return ctx.enter_context(nc.sbuf_tensor(name, shape, dt))

        def sem(name):
            return ctx.enter_context(nc.semaphore(name))

        RING = 8
        BANKS = 4
        LAG = 4
        GENS = 3

        u1 = sb("u1", [P, 2, NK, R], F32R)
        v1 = sb("v1", [P, 2, FF], F32R)
        u2 = sb("u2", [P, 2, NF, R], F32R)
        v2 = sb("v2", [P, 2, D], F32R)
        u1_raw = sb("u1_raw", [P, NK, R])
        v1_raw = sb("v1_raw", [P, FF])
        u2_raw = sb("u2_raw", [P, NF, R])
        v2_raw = sb("v2_raw", [P, D])
        b1c = sb("b1c", [P, NF])
        b2_row = sb("b2_row", [1, D])
        b2_all = sb("b2_all", [P, D])
        ones_row = sb("ones_row2", [1, P])
        ident = sb("ident2", [P, P])
        xa = sb("xa", [P, NT, D])
        xn = sb("xn", [P, NT, D])
        y = sb("y", [P, NT, D])
        xnT = sb("xn2T", [P, 2, NK, S], F32R)
        pT = sb("pT", [P, 2, S], F32R)
        qT = sb("qT", [P, 2, S], F32R)
        gelu = sb("gelu", [P, RING, S])
        hT = sb("hT", [P, RING, 2, S], F32R)
        stats = sb("stats2", [P, NT, 6])
        mv = sb("mv2", [P, NT, 2])
        rstd = sb("rstd2", [P, NT])
        varp = sb("varp2", [P, NT])
        minus_half = sb("minus_half2", [P, NT])

        psum = [ctx.enter_context(nc.psum_tensor(f"psf{i}", [P, 512], FP32)) for i in range(8)]
        h_ps, gen_ps, q_ps = psum[0:BANKS], psum[BANKS:BANKS + GENS], psum[7]

        w_loaded = [sem(f"f_w_loaded{i}") for i in range(4)]
        small_loaded = sem("f_small_loaded")
        const_step = sem("f_const_step")
        const_made = sem("f_const_made")
        x_loaded = sem("f_x_loaded")
        w_rounded = sem("f_w_rounded")
        w_split = sem("f_w_split")
        gen_ready = sem("f_gen_ready")
        rounded = sem("f_rounded")
        evacuated = sem("f_evacuated")
        h_ready = sem("h_ready")
        gelu_done = sem("gelu_done")
        h_rounded = sem("h_rounded")
        h_split = sem("h_split")
        h_used = sem("h_used")
        q_rounded = sem("q_rounded")
        q_split = sem("q_split")
        stats_done = sem("f_stats_done")
        mv_done = sem("f_mv_done")
        var_done = sem("f_var_done")
        rstd_done = sem("f_rstd_done")
        normed = sem("f_normed")
        y_ready = sem("y_ready")
        stored = sem("stored")

        FIRST = ["b2"] + [("x", t) for t in range(NT)] + ["p"]
        STEP = [("x", t) for t in range(NT)] + ["p"] + [("o", t) for t in range(NT)]
        assert len(FIRST) % GENS == 0 and len(STEP) % GENS == 0
        LAST = [("o", t) for t in range(NT)]

        def use(j, last, key):
            if j is None:
                return FIRST.index(key)
            return j * len(STEP) + (len(FIRST) + (LAST if last else STEP).index(key))

        def bank(j, last, key):
            l = FIRST if j is None else LAST if last else STEP
            return gen_ps[l.index(key) % GENS]

        def splits(j, t):
            return t if j is None else j * (NT + 1) + (NT + 1 + t)

        T_AT = {12: 0, 13: 1, 14: 2, 15: 3}

        block = ctx.enter_context(nc.Block())

        @block.sync
        def _(sp):
            def load(j):
                sp.dma_start(xa[:, :, :], x1_dram[bass.ds(j, 1), :, :].rearrange("a (t p) d -> p (a t) d", p=P)).then_inc(x_loaded, 16)

            load(0)
            sp.dma_start(u1_raw[:, :, :], U1.rearrange("(k p) r -> p k r", p=P)).then_inc(w_loaded[0], 16)
            sp.dma_start(b2_row[:, :], b2.rearrange("(a n) -> a n", a=1)).then_inc(small_loaded, 16)
            sp.dma_start(b1c[:, :], b1.rearrange("(m p) -> p m", p=P), allow_slow_non_contiguous=True).then_inc(small_loaded, 16)
            sp.dma_start(v1_raw[:, :], V1).then_inc(w_loaded[1], 16)
            sp.dma_start(u2_raw[:, :, :], U2.rearrange("(m p) r -> p m r", p=P)).then_inc(w_loaded[2], 16)
            sp.dma_start(v2_raw[:, :], V2).then_inc(w_loaded[3], 16)

            def step(j, last):
                if not last:
                    sp.wait_ge(y_ready, j * NT + NT)
                    load(j + 1)
                for t in range(NT):
                    sp.wait_ge(evacuated, use(j, last, ("o", t)) + 1)
                    sp.dma_start(out[bass.ds(j, 1), t * P:(t + 1) * P, :].rearrange("a p d -> (a p) d"),
                                 y[:, t, :]).then_inc(stored, 16)

            with sp.Fori(0, B - 1) as j:
                step(j, False)
            step(B - 1, True)
            sp.wait_ge(stored, 16 * NT * B)

        @block.gpsimd
        def _(pool):
            pool.memset(ident[:, :], 0.0).then_inc(const_step, 1)
            pool.memset(ones_row[:, :], 1.0).then_inc(const_step, 1)
            pool.memset(minus_half[:, :], -0.5).then_inc(const_step, 1)
            pool.wait_ge(const_step, 3)
            pool.affine_select(out=ident[:, :], in_=ident[:, :], compare_op=ALU.not_equal, fill=1.0,
                               base=0, pattern=[[-1, P]], channel_multiplier=1).then_inc(const_made, 1)

            def rstds(done):
                wait_apart(pool, const_step, 3, mv_done, done * NT + NT)
                pool.tensor_scalar(varp[:, :], mv[:, :, 1], EPS, None, ALU.add).then_inc(var_done, 1)
                pool.wait_ge(var_done, done + 1)
                pool.tensor_tensor(rstd[:, :], varp[:, :], minus_half[:, :], ALU.pow).then_inc(rstd_done, 1)

            rstds(0)

            def step(j, last):
                pool.wait_ge(x_loaded, j * 16 + 16)
                pool.wait_ge(normed, j * NT + NT)
                pool.wait_ge(evacuated, 1)
                if not (isinstance(j, int) and j == 0):
                    pool.wait_ge(stored, j * (16 * NT))
                for t in range(NT):
                    pool.tensor_tensor(y[:, t, :], xa[:, t, :], b2_all[:, :], ALU.add).then_inc(y_ready, 1)
                if not last:
                    rstds(j + 1)

            step(0, False)
            with pool.Fori(1, B - 1) as j:
                step(j, False)
            step(B - 1, True)

        @block.scalar
        def _(act):
            def tile_hi(j, t):
                act.wait_ge(gen_ready, use(j, False, ("x", t)) + 1)
                nc.scalar.activation(xnT[:, 0, :, t * P:(t + 1) * P],
                                     bank(j, False, ("x", t))[:, :].rearrange("p (k t) -> p k t", k=NK), ACT.Copy).then_inc(rounded, 1)

            def p_hi(j):
                act.wait_ge(gen_ready, use(j, False, "p") + 1)
                nc.scalar.activation(pT[:, 0, :], bank(j, False, "p")[:, :], ACT.Copy).then_inc(rounded, 1)

            act.wait_ge(w_loaded[0], 16)
            nc.scalar.activation(u1[:, 0, :, :], u1_raw[:, :, :], ACT.Copy).then_inc(w_rounded, 1)
            for t in range(NT):
                tile_hi(None, t)
            act.wait_ge(w_loaded[1], 16)
            nc.scalar.activation(v1[:, 0, :], v1_raw[:, :], ACT.Copy).then_inc(w_rounded, 1)
            p_hi(None)
            act.wait_ge(w_loaded[2], 16)
            nc.scalar.activation(u2[:, 0, :, :], u2_raw[:, :, :], ACT.Copy).then_inc(w_rounded, 1)
            act.wait_ge(w_loaded[3], 16)
            nc.scalar.activation(v2[:, 0, :], v2_raw[:, :], ACT.Copy).then_inc(w_rounded, 1)
            act.wait_ge(small_loaded, 32)

            def step(j, last):
                tiles = j * NF
                for m in range(NF + 1):
                    if m < NF:
                        act.wait_ge(h_ready, tiles + m + 1)
                        if not (isinstance(j, int) and j == 0 and m < RING):
                            act.wait_ge(h_split, tiles + m + 1 - RING)
                        nc.scalar.activation(gelu[:, m % RING, :], h_ps[m % BANKS][:, :], ACT.Gelu_apprx_tanh,
                                             bias=b1c[:, m:m + 1]).then_inc(gelu_done, 1)
                    if m >= 1:
                        n = m - 1
                        act.wait_ge(gelu_done, tiles + n + 1)
                        if not (isinstance(j, int) and j == 0 and n < RING):
                            act.wait_ge(h_used, tiles + n + 1 - RING)
                        nc.scalar.activation(hT[:, n % RING, 0, :], gelu[:, n % RING, :], ACT.Copy).then_inc(h_rounded, 1)
                    if not last and m - 1 in T_AT:
                        tile_hi(j, T_AT[m - 1])
                act.wait_ge(h_used, tiles + NF)
                nc.scalar.activation(qT[:, 0, :], q_ps[:, :], ACT.Copy).then_inc(q_rounded, 1)
                if not last:
                    p_hi(j)

            step(0, False)
            with act.Fori(1, B - 1) as j:
                step(j, False)
            step(B - 1, True)

        @block.vector
        def _(dve):
            def minus(out, whole, hi_half):
                return nc.vector.tensor_tensor(out, whole, hi_half.bitcast(FP32), ALU.subtract)

            def tile_lo(j, t):
                dve.wait_ge(rounded, splits(j, t) + 1)
                cols = slice(t * P, (t + 1) * P)
                minus(xnT[:, 1, :, cols], bank(j, False, ("x", t))[:, :].rearrange("p (k t) -> p k t", k=NK),
                      xnT[:, 0, :, cols]).then_inc(evacuated, 1)

            def p_lo(j):
                dve.wait_ge(rounded, splits(j, NT) + 1)
                minus(pT[:, 1, :], bank(j, False, "p")[:, :], pT[:, 0, :]).then_inc(evacuated, 1)

            def norm_stats(done):
                dve.wait_ge(x_loaded, done * 16 + 16)
                for t in range(NT):
                    nc.vector.bn_stats(stats[:, t, :], xa[:, t, :]).then_inc(stats_done, 1)
                for t in range(NT):
                    wait_apart(dve, const_made, 1, stats_done, done * NT + t + 1)
                    nc.vector.bn_aggr(mv[:, t, :], stats[:, t, :]).then_inc(mv_done, 1)

            def normalise(done):
                dve.wait_ge(rstd_done, done + 1)
                for t in range(NT):
                    nc.vector.tensor_scalar(xn[:, t, :], xa[:, t, :], mv[:, t, 0:1], rstd[:, t:t + 1],
                                            ALU.subtract, ALU.mult).then_inc(normed, 1)

            dve.wait_ge(gen_ready, 1)
            nc.vector.tensor_copy(b2_all[:, :], bank(None, False, "b2")[:, :]).then_inc(evacuated, 1)
            norm_stats(0)
            dve.wait_ge(w_rounded, 1)
            minus(u1[:, 1, :, :], u1_raw[:, :, :], u1[:, 0, :, :]).then_inc(w_split, 1)
            normalise(0)
            for t in range(NT):
                tile_lo(None, t)
            dve.wait_ge(w_rounded, 2)
            minus(v1[:, 1, :], v1_raw[:, :], v1[:, 0, :]).then_inc(w_split, 1)
            p_lo(None)
            dve.wait_ge(w_rounded, 3)
            minus(u2[:, 1, :, :], u2_raw[:, :, :], u2[:, 0, :, :]).then_inc(w_split, 1)
            dve.wait_ge(w_rounded, 4)
            minus(v2[:, 1, :], v2_raw[:, :], v2[:, 0, :]).then_inc(w_split, 1)

            def step(j, last):
                tiles = j * NF
                for m in range(NF):
                    dve.wait_ge(h_rounded, tiles + m + 1)
                    minus(hT[:, m % RING, 1, :], gelu[:, m % RING, :], hT[:, m % RING, 0, :]).then_inc(h_split, 1)
                    if not last:
                        if m == 9:
                            norm_stats(j + 1)
                        if m == 11:
                            normalise(j + 1)
                        if m in T_AT:
                            tile_lo(j, T_AT[m])
                dve.wait_ge(q_rounded, j + 1)
                minus(qT[:, 1, :], q_ps[:, :], qT[:, 0, :]).then_inc(q_split, 1)
                if not last:
                    p_lo(j)
                for t in range(NT):
                    dve.wait_ge(gen_ready, use(j, last, ("o", t)) + 1)
                    dve.wait_ge(y_ready, j * NT + t + 1)
                    nc.vector.tensor_tensor(y[:, t, :], bank(j, last, ("o", t))[:, :], y[:, t, :], ALU.add).then_inc(evacuated, 1)

            step(0, False)
            with dve.Fori(1, B - 1) as j:
                step(j, False)
            step(B - 1, True)

        @block.tensor
        def _(pe):
            def claim(j, last, key):
                n = use(j, last, key)
                if j is not None or n >= GENS:
                    pe.wait_ge(evacuated, n - GENS + 1)
                return bank(j, last, key)

            def summed(ps, terms):
                for n, (left, right) in enumerate(terms):
                    done = nc.tensor.matmul(ps[:, :], left, right, start=(n == 0), stop=(n == len(terms) - 1))
                return done

            def tile(j, t, batch):
                ps = claim(j, False, ("x", t))
                pe.wait_ge(normed, batch * NT + (t + 1))
                for k in range(NK):
                    done = nc.tensor.transpose(ps[:, k * P:(k + 1) * P], xn[:, t, k * P:(k + 1) * P], ident[:, :])
                done.then_inc(gen_ready, 1)

            def first_product(j):
                ps = claim(j, False, "p")
                pe.wait_ge(evacuated, use(j, False, ("x", NT - 1)) + 1)
                summed(ps, [(u1[:, i, k, :], xnT[:, i2, k, :]) for k in range(NK) for i, i2 in TERMS]).then_inc(gen_ready, 1)

            pe.wait_ge(const_made, 1)
            pe.wait_ge(small_loaded, 32)
            nc.tensor.matmul(bank(None, False, "b2")[:, :], ones_row[:, :], b2_row[:, :], start=True, stop=True).then_inc(gen_ready, 1)
            for t in range(NT):
                tile(None, t, 0)
            pe.wait_ge(w_split, 1)
            first_product(None)
            pe.wait_ge(w_split, 4)

            def step(j, last):
                tiles = j * NF
                pe.wait_ge(evacuated, (use(None, False, "p") if isinstance(j, int) and j == 0 else use(j - 1, False, "p")) + 1)
                for m in range(NF + LAG):
                    if m < NF:
                        if not (isinstance(j, int) and j == 0 and m < BANKS):
                            pe.wait_ge(gelu_done, tiles + m + 1 - BANKS)
                        summed(h_ps[m % BANKS], [(v1[:, i, m * P:(m + 1) * P], pT[:, i2, :]) for i, i2 in TERMS]).then_inc(h_ready, 1)
                    if m >= LAG:
                        n = m - LAG
                        if n == 0 and not (isinstance(j, int) and j == 0):
                            pe.wait_ge(q_split, j)
                        pe.wait_ge(h_split, tiles + n + 1)
                        for i, (w, a) in enumerate(TERMS):
                            done = nc.tensor.matmul(q_ps[:, :], u2[:, w, n, :], hT[:, n % RING, a, :],
                                                    start=(n == 0 and i == 0), stop=(n == NF - 1 and i == 2))
                        done.then_inc(h_used, 1)
                    if not last and m in T_AT:
                        tile(j, T_AT[m], j + 1)
                if not last:
                    first_product(j)
                pe.wait_ge(q_split, j + 1)
                for t in range(NT):
                    ps = claim(j, last, ("o", t))
                    summed(ps, [(qT[:, i, t * P:(t + 1) * P], v2[:, i2, :]) for i, i2 in TERMS]).then_inc(gen_ready, 1)

            step(0, False)
            with pe.Fori(1, B - 1) as j:
                step(j, False)
            step(B - 1, True)


_INS = ["x", "ctx_1024", "L0_xattn_Wq", "L0_xattn_bq", "L0_xattn_Wk", "L0_xattn_bk", "L0_xattn_Wv", "L0_xattn_bv",
        "L0_xattn_Wo", "L0_xattn_bo", "L0_ffn_U1", "L0_ffn_V1", "L0_ffn_b1", "L0_ffn_U2", "L0_ffn_V2", "L0_ffn_b2"]


def build(nc, a, out):
    x1_dram = nc.dram_tensor("x1_scratch", (B, S, D), FP32).ap()
    attention_phase(nc, a["x"], a["ctx_1024"], *(a[f"L0_xattn_{n}"] for n in ("Wq", "bq", "Wk", "bk", "Wv", "bv", "Wo", "bo")), x1_dram)
    ffn_phase(nc, x1_dram, *(a[f"L0_ffn_{n}"] for n in ("U1", "V1", "b1", "U2", "V2", "b2")), out)


def kernel(**inputs):
    import numpy as _np
    import concourse.bacc as _bacc
    from concourse.bass_utils import run_bass_kernel_spmd as _run

    nc = _bacc.Bacc("TRN2", target_bir_lowering=False, num_devices=1)
    arrays, args = {}, {}
    for name in _INS:
        a = _np.ascontiguousarray(inputs[name])
        arrays[f"in_{name}_dram"] = a
        args[name] = nc.dram_tensor(f"in_{name}_dram", a.shape, mybir.dt.from_np(a.dtype), kind="ExternalInput").ap()
    out = nc.dram_tensor("out_0_dram", (B, S, D), FP32, kind="ExternalOutput").ap()
    build(nc, args, out)
    r = _run(nc, [arrays], core_ids=[0])
    return r.results[0]["out_0_dram"]
```

```python
import concourse.bass as bass
from concourse import mybir
from contextlib import ExitStack

FP32 = mybir.dt.float32
F32R = mybir.dt.float32r
BF16 = mybir.dt.bfloat16
ALU = mybir.AluOpType
ACT = mybir.ActivationFunctionType
AXIS_X = mybir.AxisListType.X

B, S, D = 8, 512, 512
P = 128
H, HD = 16, 32
NT = S // P
NK = D // P
HG = P // HD
NG = H // HG
FF, R = 2048, 128
NF = FF // P
EPS = 1e-5
SCALE = 1.0 / (HD ** 0.5)
MASKED = -3.0e38
UNITS = 10
A_UNITS, B_UNITS = HG, HG

TERMS = ((0, 0), (0, 1), (1, 0))


def wait_apart(eng, met, count, sem, value):
    if not isinstance(value, int):
        value = eng.to_reg(value)
    eng.wait_ge(met, count)
    eng.wait_ge(sem, value)


class Kept:

    def __init__(self, nc, ctx):
        def sb(name, shape, dt=FP32):
            return ctx.enter_context(nc.sbuf_tensor(name, shape, dt))

        self.wqT = sb("wqT", [P, 2, NK, D], F32R)
        self.wkT = sb("wkT", [P, 2, NK, D], F32R)
        self.wvT = sb("wvT", [P, 2, NK, D], F32R)
        with ExitStack() as early:
            self.xnT = early.enter_context(nc.sbuf_tensor("xnT", [P, 2, NK, S], F32R))
            self.cxT = early.enter_context(nc.sbuf_tensor("cxT", [P, 2, NK, S], F32R))
        self.v1_raw = sb("v1_raw", [P, FF])
        self.u2_raw = sb("u2_raw", [P, NF, R])
        self.u1_raw = sb("u1_raw", [P, NK, R])
        self.v2_raw = sb("v2_raw", [P, D])
        self.xn = sb("xn_first", [P, NT, D])
        self.b2_row = sb("b2_row", [1, D])
        self.spare = sb("spare", [P, D])
        self.vc = sb("vc", [P, 2, NT, D])
        self.ident = sb("ident", [P, P])
        self.ones_row = sb("ones_row", [1, P])
        self.minus_half = sb("minus_half", [P, NT])
        self.b1c = sb("b1c", [P, NF])
        self.v1 = self.wqT[:, :, :, :].rearrange("p i k n -> p i (k n)")
        self.u2 = self.wkT[:, :, :, :].rearrange("p i k (m r) -> p i (k m) r", r=R)
        self.u1 = self.wvT[:, :, 0, :].rearrange("p i (k r) -> p i k r", r=R)
        self.v2 = self.wvT[:, :, 1, :]
        self.xa = self.vc[:, 0, :, :]


def attention_phase(nc, kept, x, ctx_in, Wq, bq, Wk, bk, Wv, bv, Wo, bo, x1_dram, U1, V1, b1, U2, V2, b2):
    with ExitStack() as ctx:
        def sb(name, shape, dt=FP32):
            return ctx.enter_context(nc.sbuf_tensor(name, shape, dt))

        def sem(name):
            return ctx.enter_context(nc.semaphore(name))

        wqT, wkT, wvT, xnT, cxT, vc = kept.wqT, kept.wkT, kept.wvT, kept.xnT, kept.cxT, kept.vc
        ident, ones_row, minus_half = kept.ident, kept.ones_row, kept.minus_half
        woT = sb("woT", [P, 2, NK, D], F32R)
        attnT = sb("attnT", [P, 2, NK, S], F32R)
        QLO, QHI, KHI, KLO = range(4)
        qk = sb("qk", [P, 4, S], F32R)
        M_ROW = 3 * HD
        qs = sb("qs", [P, 2, 2, HG, S], F32R)
        probs = sb("probs", [P, UNITS, S])
        xbuf = sb("xbuf", [P, NT, D])
        attn = sb("attn", [P, S])
        max_split = sb("max_split", [P, NT, 2, HG])
        mrow = sb("mrow", [2 * HG, S], F32R)
        negmax = sb("negmax", [P, NT, HG])
        bo_all = sb("bo_all", [P, D])
        ident16 = sb("ident16", [P, P], BF16)
        mask16 = sb("mask16", [P, P], BF16)
        ones32 = sb("ones32", [P, HD])
        bqc = sb("bqc", [P, NK])
        bkc = sb("bkc", [P, NK])
        bvc = sb("bvc", [P, NK])
        stats = sb("stats", [P, NT, 6])
        mv = sb("mv", [P, NT, 2])
        rstd = sb("rstd", [P, NT])
        varp = sb("varp", [P, NT])

        ff_weights = ((kept.v1, V1, kept.v1_raw[:, :]),
                      (kept.u2, U2.rearrange("(m p) r -> p m r", p=P), kept.u2_raw[:, :, :]),
                      (kept.u1, U1.rearrange("(k p) r -> p k r", p=P), kept.u1_raw[:, :, :]),
                      (kept.v2, V2, kept.v2_raw[:, :]))

        psum = [ctx.enter_context(nc.psum_tensor(f"ps{i}", [P, 512], FP32)) for i in range(8)]
        score_ps, max_ps, gen_ps, out_ps, den_ps = psum[0:2], psum[2:4], psum[4:6], psum[6], psum[7]

        w_loaded = [sem(f"w_loaded{i}") for i in range(4)]
        small_loaded = sem("small_loaded")
        ff_loaded = [sem(f"ff_loaded{i}") for i in range(4)]
        ff_small_loaded = sem("ff_small_loaded")
        ff_rounded = sem("ff_rounded")
        ff_split = sem("ff_split")
        xa_loaded = sem("xa_loaded")
        bo_loaded = sem("bo_loaded")
        ident_made = sem("ident_made")
        const_step = sem("const_step")
        stack_made = sem("stack_made")
        w_ready = sem("w_ready")
        w_rounded = sem("w_rounded")
        w_split = sem("w_split")
        max_hi = sem("max_hi")
        max_lo = sem("max_lo")
        x_loaded = sem("x_loaded")
        ctx_loaded = sem("ctx_loaded")
        gen_ready = sem("gen_ready")
        rounded = sem("rounded")
        emptied = [sem(f"emptied{i}") for i in range(2)]
        stacked = sem("stacked")
        m_stacked = sem("m_stacked")
        max_ready = sem("max_ready")
        max_done = sem("max_done")
        score_ready = sem("score_ready")
        exp_done = sem("exp_done")
        masked = sem("masked")
        folded = sem("folded")
        av0_done = sem("av0_done")
        av_done = sem("av_done")
        recip_done = sem("recip_done")
        attn_scaled = sem("attn_scaled")
        attn_rounded = sem("attn_rounded")
        attn_ready = sem("attn_ready")
        stats_done = sem("stats_done")
        mv_done = sem("mv_done")
        var_done = sem("var_done")
        rstd_done = sem("rstd_done")
        normed = sem("normed")
        residual_ready = sem("residual_ready")
        x1_stored = sem("x1_stored")

        def keys(name, n=NT):
            return [(name, t) for t in range(n)]

        AHEAD = (keys("c") + [("k", -2)] + keys("x") + [("q", -2), ("bo",), ("v", 0), ("v", 1),
                                                        ("k", -1), ("q", -1), ("m", -1), ("v", 2), ("v", 3)])

        def with_scores(kind, g):
            if kind == "last" and g >= 2:
                return []
            outs = [] if kind == "first" else [("o", 2), ("o", 3)]
            return [[("q", 0)], outs + [("q", 1)], [("v", 0), ("c", 2), ("v", 1), ("c", 3)] + keys("x"), [("v", 2), ("q", 3)]][g]

        def with_maxima(kind, g):
            if kind == "last" and g >= 2:
                return []
            outs = [] if kind == "first" else [("o", 0)]
            return [[("k", 0)] + outs, [("k", 1)], [("k", 2), ("q", 2)], [("k", 3)]][g]

        def at_end(kind, g):
            return [[] if kind == "first" else [("o", 1)], [] if kind == "last" else [("c", 0), ("c", 1)],
                    [], [] if kind == "last" else [("v", 3)]][g]

        def in_step(kind):
            uses = []
            for g in range(NG):
                uses += with_scores(kind, g) + with_maxima(kind, g)
                if looks_ahead(kind, g):
                    uses.append(("m", g))
                uses += at_end(kind, g)
            return uses

        def products_by(kind, g):
            return 12 if g == 1 else 9 if with_maxima(kind, g)[1:] else 8

        def k_at(kind, g):
            return 5 if with_maxima(kind, g)[1:] else 7

        def projects(kind, g):
            return not (kind == "last" and g >= 2)

        def looks_ahead(kind, g):
            return not (kind == "last" and g == NG - 1)

        def uses_of(kind):
            return {"ahead": AHEAD, "tail": in_step("last") + [("tail", t) for t in range(NT)]}.get(kind) or in_step(kind)

        def before(b, kind, width):
            if kind == "ahead":
                return 0
            if kind == "first":
                return width(AHEAD)
            sofar = width(AHEAD) + width(in_step("first"))
            if kind in ("last", "tail"):
                return sofar + (B - 2) * width(in_step("mid"))
            return b * width(in_step("mid")) + (sofar - width(in_step("mid")))

        def both(kind, g):
            return ("q", g) if g == 2 else ("k", g)

        SPLIT = "cxqk"

        def splits(l):
            return sum(u[0] in SPLIT for u in l)

        def use(b, kind, key):
            return before(b, kind, len) + uses_of(kind).index(key)

        def split(b, kind, key):
            l = uses_of(kind)
            return before(b, kind, splits) + splits(l[:l.index(key)])

        def bank_of(kind, key):
            return uses_of(kind).index(key) % 2

        def bank(kind, key):
            return gen_ps[bank_of(kind, key)]

        def bank_use(b, kind, key):
            return before(b, kind, lambda l: len(l) // 2) + uses_of(kind).index(key) // 2

        def has_left(b, kind, key):
            return emptied[bank_of(kind, key)], bank_use(b, kind, key) + 1

        assert B % 2 == 0
        for kind in ("ahead", "first", "mid"):
            assert len(uses_of(kind)) % 2 == 0

        def steps(eng, step):
            step(0, "first")
            with eng.Fori(0, (B - 2) // 2) as pair:
                step(pair * 2 + 1, "mid", 1)
                step(pair * 2 + 2, "mid", 0)
            step(B - 1, "last")

        def unit(u):
            if u < A_UNITS:
                return "A", u
            if u < A_UNITS + B_UNITS:
                return "B", u - A_UNITS
            return "C", u - A_UNITS - B_UNITS

        K_LO, K_MID, K_HI = P, 2 * P, 3 * P
        GROUP = NG * UNITS
        V1_BY = 6
        X_AT, X_LATE = (7, 9), {0: 2, 1: 3}
        ATTN_AT = 7
        AV0_AT, AV1_AT = 1, 9
        LEAD = (4, 12, 0, 12)
        STACK_DMAS = 3 * HG
        weight_ps = score_ps + max_ps + [out_ps, den_ps]
        WEIGHTS = ((wkT, probs[:, 0:NK, :]), (wqT, probs[:, NK:2 * NK, :]), (wvT, vc[:, 1, :, :]), (woT, probs[:, 0:NK, :]))

        block = ctx.enter_context(nc.Block())

        @block.sync
        def _(sp):
            def load_weight(i, w):
                sp.dma_start(WEIGHTS[i][1], w.rearrange("(m p) n -> p m n", p=P)).then_inc(w_loaded[i], 16)

            def load_tokens(to, of, b, loaded):
                sp.dma_start(to, of[bass.ds(b, 1), :, :].rearrange("a (t p) d -> p (a t) d", p=P)).then_inc(loaded, 16)

            def stack(slot, heads=range(HG)):
                for h in heads:
                    rows = slice(h * HD, (h + 1) * HD)
                    for row, pair in enumerate((slice(QHI, KHI + 1), slice(QLO, KHI + 1, 2), slice(QHI, KLO + 1, 2))):
                        sp.dma_start(qs[row * HD:(row + 1) * HD, slot, :, h, :].bitcast(FP32),
                                     qk[rows, pair, :].bitcast(FP32)).then_inc(stacked, 16)

            def stack_max(slot):
                for half in range(2):
                    sp.dma_start(qs[M_ROW + half:M_ROW + half + 1, slot, 0, :, :].bitcast(FP32),
                                 mrow[half * HG:(half + 1) * HG, :].bitcast(FP32)).then_inc(m_stacked, 16)

            def store_x1(b, at, kind, tiles):
                for t in tiles:
                    sp.wait_ge(*has_left(at, kind, ("tail" if kind == "tail" else "o", t)))
                    sp.dma_start(x1_dram[bass.ds(b, 1), t * P:(t + 1) * P, :].rearrange("a p d -> (a p) d"),
                                 xbuf[:, t, :]).then_inc(x1_stored, 16)

            load_tokens(vc[:, 0, :, :], ctx_in, 0, ctx_loaded)
            load_weight(0, Wk)
            load_tokens(xbuf[:, :, :], x, 0, x_loaded)
            for b_, c in ((bq, bqc), (bk, bkc), (bv, bvc)):
                sp.dma_start(c[:, :], b_.rearrange("(m p) -> p m", p=P), allow_slow_non_contiguous=True).then_inc(small_loaded, 16)
            load_weight(1, Wq)
            sp.dma_start(attn[0:1, :], bo.rearrange("(a n) -> a n", a=1)).then_inc(bo_loaded, 16)
            load_weight(2, Wv)
            sp.wait_ge(w_ready, NK)
            load_weight(3, Wo)
            sp.wait_ge(stack_made, 4)
            for n in (0, 1):
                sp.wait_ge(*has_left(None, "ahead", ("k", n - 2)))
                sp.wait_ge(*has_left(None, "ahead", ("q", n - 2)))
                stack(n)
            sp.wait_ge(*has_left(None, "ahead", ("m", -1)))
            stack_max(0)

            def step(b, kind, odd=None):
                if kind == "first":
                    sp.wait_ge(w_ready, 3 * NK)
                    sp.wait_ge(gen_ready, use(None, "ahead", ("x", NT - 1)) + 1)
                    load_tokens(xbuf[:, :, :], x, b + 1, x_loaded)
                odd = b % 2 if odd is None else odd
                if kind == "first":
                    load_tokens(vc[:, 1 - odd, :, :], ctx_in, b + 1, ctx_loaded)
                elif kind != "last":
                    wait_apart(sp, stack_made, 4, av_done, b * NG)
                    load_tokens(vc[:, 1 - odd, :, :], ctx_in, b + 1, ctx_loaded)
                for g in range(NG):
                    if g == 1 and kind != "first":
                        store_x1(b - 1, b, kind, (2, 3))
                        sp.wait_ge(x1_stored, b * (16 * NT))
                        load_tokens(xbuf[:, :, :], x, (b + 1) if kind == "mid" else b, x_loaded)
                    if g == 2 and kind != "last":
                        sp.wait_ge(gen_ready, use(b, kind, ("x", NT - 1)) + 1)
                        load_tokens(xbuf[:, :, :], x, b, x_loaded)
                    if projects(kind, g) and g != 1:
                        wait_apart(sp, stack_made, 4, score_ready, b * GROUP + UNITS * (g + 1))
                        sp.wait_ge(*has_left(b, kind, both(kind, g)))
                        stack(g % 2, range(1))
                    if looks_ahead(kind, g):
                        sp.wait_ge(*has_left(b, kind, ("m", g)))
                        stack_max((g + 1) % 2)
                    if projects(kind, g) and g != 1:
                        stack(g % 2, range(1, HG))
                    elif projects(kind, g):
                        wait_apart(sp, stack_made, 4, score_ready, b * GROUP + UNITS * (g + 1))
                        sp.wait_ge(*has_left(b, kind, both(kind, g)))
                        stack(g % 2)
                    if g == 1 and kind == "last":
                        sp.wait_ge(gen_ready, use(b, kind, ("k", 1)) + 1)
                        for i, (_, w, raw) in enumerate(ff_weights):
                            sp.dma_start(raw, w).then_inc(ff_loaded[i], 16)
                        for t in range(NT):
                            sp.dma_start(kept.xa[:, t, :], x1_dram[0:1, t * P:(t + 1) * P, :].rearrange("a p d -> (a p) d")).then_inc(xa_loaded, 16)
                        sp.dma_start(kept.b2_row[:, :], b2.rearrange("(a n) -> a n", a=1)).then_inc(ff_small_loaded, 16)
                        sp.dma_start(kept.b1c[:, :], b1.rearrange("(m p) -> p m", p=P), allow_slow_non_contiguous=True).then_inc(ff_small_loaded, 16)
                    if g == 0 and kind != "first":
                        store_x1(b - 1, b, kind, (0, 1))

            steps(sp, step)
            store_x1(B - 1, None, "tail", range(NT))
            sp.wait_ge(x1_stored, 16 * NT * B)
            sp.wait_ge(ff_small_loaded, 32)

        @block.gpsimd
        def _(pool):
            pool.memset(ident[:, :], 0.0).then_inc(const_step, 1)
            pool.wait_ge(const_step, 1)
            pool.affine_select(out=ident[:, :], in_=ident[:, :], compare_op=ALU.not_equal, fill=1.0,
                               base=0, pattern=[[-1, P]], channel_multiplier=1).then_inc(ident_made, 1)
            pool.memset(minus_half[:, :], -0.5).then_inc(const_step, 1)
            pool.memset(mask16[:, :], 0.0).then_inc(const_step, 1)
            pool.memset(ones32[:, :], 1.0).then_inc(const_step, 1)
            pool.memset(ones_row[:, :], 1.0).then_inc(const_step, 1)
            pool.wait_ge(const_step, 5)
            pool.affine_select(out=mask16[:, :], in_=mask16[:, :], compare_op=ALU.is_ge, fill=MASKED,
                               base=0, pattern=[[-1, P]], channel_multiplier=1).then_inc(const_step, 1)
            pool.wait_ge(ident_made, 1)
            pool.tensor_copy(ident16[:, :], ident[:, :]).then_inc(const_step, 1)

            def rstds(done):
                wait_apart(pool, const_step, 2, mv_done, done * NT + NT)
                pool.tensor_scalar(varp[:, :], mv[:, :, 1], EPS, None, ALU.add).then_inc(var_done, 1)
                pool.wait_ge(var_done, done + 1)
                pool.tensor_tensor(rstd[:, :], varp[:, :], minus_half[:, :], ALU.pow).then_inc(rstd_done, 1)

            pool.wait_ge(const_step, 7)
            for slot in range(2):
                pool.memset(qs[M_ROW:P, slot, :, :, :].bitcast(FP32), 0.0).then_inc(stack_made, 1)
            pool.wait_ge(stack_made, 2)
            for slot in range(2):
                pool.memset(qs[M_ROW:M_ROW + 2, slot, 1, :, :].bitcast(FP32), 1.0).then_inc(stack_made, 1)
            pool.wait_ge(stack_made, 4)
            rstds(0)

            def causal(view):
                pool.affine_select(out=view, in_=view, compare_op=ALU.is_ge, fill=0.0, base=0,
                                   pattern=[[0, HG], [1, P]], channel_multiplier=-1).then_inc(masked, 1)

            pa, pb, pc = probs[:, 0:HG, :], probs[:, HG:2 * HG, :], probs[:, 2 * HG:UNITS, :]
            pc4 = pc.rearrange("p c (h q) -> p (c h) q", h=2)

            def step(b, kind, odd=None):
                for g in range(NG):
                    grp = b * NG + g
                    units = b * GROUP + g * UNITS
                    wait_apart(pool, const_step, 7, exp_done, units + A_UNITS)
                    causal(pa[:, :, 0:P])
                    wait_apart(pool, const_step, 7, exp_done, units + A_UNITS + B_UNITS)
                    causal(pb[:, :, 0:P])
                    causal(pb[:, :, K_HI:S])
                    wait_apart(pool, const_step, 7, exp_done, units + UNITS)
                    causal(pc4[:, :, 0:P])
                    if not (kind == "last" and g == NG - 1):
                        pool.wait_ge(av0_done, grp + 1)
                        pool.wait_ge(masked, grp * 4 + 4)
                        pool.tensor_tensor(pa[:, :, K_LO:S], pa[:, :, K_LO:S], pb[:, :, 0:S - K_LO], ALU.add).then_inc(folded, 1)
                        pool.wait_ge(folded, grp * 3 + 1)
                        pool.tensor_tensor(pa[:, :, K_MID:S], pa[:, :, K_MID:S], pc4, ALU.add).then_inc(folded, 1)
                        pool.wait_ge(folded, grp * 3 + 2)
                        pool.tensor_tensor(pa[:, :, K_HI:S], pa[:, :, K_HI:S], pb[:, :, K_HI:S], ALU.add).then_inc(folded, 1)
                    if g == 1 and kind != "last":
                        rstds(b + 1)
                    if g == 3 and kind == "last":
                        rstds(B)
                    if g >= 2:
                        pool.wait_ge(x_loaded, b * 32 + (32 if kind == "last" else 48))
                        pool.wait_ge(*has_left(None, "ahead", ("bo",)))
                        for t in range((g - 2) * 2, (g - 1) * 2):
                            pool.tensor_tensor(xbuf[:, t, :], xbuf[:, t, :], bo_all[:, :], ALU.add).then_inc(residual_ready, 1)

            steps(pool, step)
            to, _, raw = ff_weights[0]
            pool.wait_ge(ff_rounded, 1)
            pool.tensor_tensor(to[:, 1], raw, to[:, 0].bitcast(FP32), ALU.subtract).then_inc(ff_split, 1)

        @block.scalar
        def _(act):
            def gen(kind, key):
                ps = bank(kind, key)
                return ps[:, :].rearrange("p (k t) -> p k t", k=NK) if key[0] in "cx" else ps[:, :]

            def hi(out, b, kind, key, bias=None):
                act.wait_ge(gen_ready, use(b, kind, key) + 1)
                if bias is None:
                    nc.scalar.activation(out, gen(kind, key), ACT.Copy).then_inc(rounded, 1)
                else:
                    nc.scalar.activation(out, gen(kind, key), ACT.Identity, bias=bias).then_inc(rounded, 1)

            def weight_hi(i):
                for k in range(NK):
                    n = i * NK + k
                    act.wait_ge(w_ready, n + 1)
                    nc.scalar.activation(WEIGHTS[i][0][:, 0, k, :], weight_ps[n % 6][:, :], ACT.Copy).then_inc(w_rounded, 1)

            def value(b, kind, t, half):
                act.wait_ge(gen_ready, use(b, kind, ("v", t)) + 1)
                nc.scalar.activation(vc[:, half, t, :], bank(kind, ("v", t))[:, :], ACT.Copy).then_inc(emptied[bank_of(kind, ("v", t))], 1)

            def maxima_out(b, kind, g):
                act.wait_ge(gen_ready, use(b, kind, ("m", g)) + 1)
                nc.scalar.activation(mrow[:, :], bank(kind, ("m", g))[0:2 * HG, :], ACT.Copy).then_inc(emptied[bank_of(kind, ("m", g))], 1)

            def token_hi(b, kind, name, t):
                hi((cxT if name == "c" else xnT)[:, 0, :, t * P:(t + 1) * P], b, kind, (name, t))

            def attn_hi(grp, g):
                act.wait_ge(attn_scaled, grp + 1)
                nc.scalar.activation(attnT[:, 0, g, :], attn[:, :], ACT.Identity, bias=bvc[:, g:g + 1]).then_inc(attn_rounded, 1)

            for t in range(NT):
                token_hi(None, "ahead", "c", t)
            weight_hi(0)
            act.wait_ge(small_loaded, 48)
            hi(qk[:, KHI, :], None, "ahead", ("k", -2), bkc[:, 0:1])
            for t in range(NT):
                token_hi(None, "ahead", "x", t)
            weight_hi(1)
            hi(qk[:, QHI, :], None, "ahead", ("q", -2), bqc[:, 0:1])
            weight_hi(2)
            weight_hi(3)
            value(None, "ahead", 0, 0)
            value(None, "ahead", 1, 0)
            act.wait_ge(stacked, 16 * STACK_DMAS)
            hi(qk[:, KHI, :], None, "ahead", ("k", -1), bkc[:, 1:2])
            hi(qk[:, QHI, :], None, "ahead", ("q", -1), bqc[:, 1:2])
            maxima_out(None, "ahead", -1)
            value(None, "ahead", 2, 0)
            value(None, "ahead", 3, 0)

            def step(b, kind, odd=None):
                other = 1 - (b % 2 if odd is None else odd)
                for g in range(NG):
                    grp = b * NG + g
                    units = b * GROUP + g * UNITS
                    mt = (g + 2) % NG
                    prepares = g == 2 and kind != "last"
                    if prepares:
                        value(b, kind, 0, other)
                        token_hi(b, kind, "c", 2)
                    if g == 3 and kind != "last":
                        value(b, kind, 2, other)
                    for u in range(UNITS):
                        act.wait_ge(score_ready, units + u + 1)
                        nc.scalar.activation(probs[:, u, :], score_ps[u % 2][:, :], ACT.Exp, scale=SCALE).then_inc(exp_done, 1)
                        if prepares and u == V1_BY - 1:
                            value(b, kind, 1, other)
                        if prepares and u == V1_BY:
                            token_hi(b, kind, "c", 3)
                        if prepares and u in X_AT:
                            token_hi(b, kind, "x", X_AT.index(u))
                        if u == ATTN_AT and not (kind == "first" and g == 0):
                            if g == 1 and kind != "first":
                                act.wait_ge(gen_ready, use(b, kind, ("o", 3)) + 1)
                            attn_hi(grp - 1, (g - 1) % NG)
                    if prepares:
                        for t in X_LATE.values():
                            token_hi(b, kind, "x", t)
                    if projects(kind, g):
                        act.wait_ge(stacked, (grp + 2) * (16 * STACK_DMAS))
                        halves = [(QHI, "q", bqc), (KHI, "k", bkc)]
                        for half, name, bias in halves[::-1] if g == 2 else halves:
                            hi(qk[:, half, :], b, kind, (name, g), bias[:, mt:mt + 1])
                    if g == 2 and kind == "last":
                        for i, (to, _, raw) in enumerate(ff_weights):
                            act.wait_ge(ff_loaded[i], 16)
                            nc.scalar.activation(to[:, 0], raw, ACT.Copy).then_inc(ff_rounded, 1)
                    if looks_ahead(kind, g):
                        maxima_out(b, kind, g)
                    if g == 1 and kind != "last":
                        token_hi(b, kind, "c", 0)
                        token_hi(b, kind, "c", 1)
                    if g == 3 and kind != "last":
                        value(b, kind, 3, other)

            steps(act, step)
            for t in range(NT):
                act.wait_ge(attn_scaled, B * NG + t)
                nc.scalar.activation(attnT[:, 0, NG - 1, t * P:(t + 1) * P], attn[:, t * P:(t + 1) * P], ACT.Identity,
                                     bias=bvc[:, NG - 1:NG]).then_inc(attn_rounded, 1)

        @block.vector
        def _(dve):
            def gen(kind, key):
                ps = bank(kind, key)
                return ps[:, :].rearrange("p (k t) -> p k t", k=NK) if key[0] in "cx" else ps[:, :]

            def lo(out, hi_half, b, kind, key, bias=None):
                dve.wait_ge(rounded, split(b, kind, key) + 1)
                hi_half = hi_half.bitcast(FP32)
                if bias is None:
                    nc.vector.tensor_tensor(out, gen(kind, key), hi_half, ALU.subtract).then_inc(emptied[bank_of(kind, key)], 1)
                else:
                    nc.vector.scalar_tensor_tensor(out, gen(kind, key), bias, hi_half, ALU.add, ALU.subtract).then_inc(emptied[bank_of(kind, key)], 1)

            def weight_lo(i):
                for k in range(NK):
                    n = i * NK + k
                    dve.wait_ge(w_rounded, n + 1)
                    nc.vector.tensor_tensor(WEIGHTS[i][0][:, 1, k, :], weight_ps[n % 6][:, :],
                                            WEIGHTS[i][0][:, 0, k, :].bitcast(FP32), ALU.subtract).then_inc(w_split, 1)

            def tile_stats(t):
                nc.vector.bn_stats(stats[:, t, :], xbuf[:, t, :]).then_inc(stats_done, 1)

            def mean_and_variance(done):
                for t in range(NT):
                    wait_apart(dve, ident_made, 1, stats_done, done * NT + t + 1)
                    nc.vector.bn_aggr(mv[:, t, :], stats[:, t, :]).then_inc(mv_done, 1)

            def normalise(done, tiles):
                dve.wait_ge(rstd_done, done + 1)
                for t in tiles:
                    nc.vector.tensor_scalar(xbuf[:, t, :], xbuf[:, t, :], mv[:, t, 0:1], rstd[:, t:t + 1],
                                            ALU.subtract, ALU.mult).then_inc(normed, 1)

            def token_lo(b, kind, name, t):
                to, cols = cxT if name == "c" else xnT, slice(t * P, (t + 1) * P)
                lo(to[:, 1, :, cols], to[:, 0, :, cols], b, kind, (name, t))

            def maxima(n_units, u):
                dve.wait_ge(max_ready, n_units + u + 1)
                kind, j = unit(u)
                ps = max_ps[u % 2]

                def take(out, in_):
                    return nc.vector.tensor_reduce(out, in_, AXIS_X, ALU.max, negate=True)

                if kind == "A":
                    take(negmax[:, 3, j:j + 1], ps[:, :]).then_inc(max_done, 1)
                elif kind == "B":
                    take(negmax[:, 0, j:j + 1], ps[:, 0:P])
                    take(negmax[:, 2, j:j + 1], ps[:, P:S]).then_inc(max_done, 1)
                else:
                    take(negmax[:, 1, 2 * j:2 * j + 2], ps[:, :].rearrange("p (h k) -> p h k", h=2)).then_inc(max_done, 1)

            def split_maxima(n):
                dve.wait_ge(max_done, n * UNITS + UNITS)
                nc.vector.tensor_copy(max_split[:, :, 0, :].bitcast(F32R), negmax[:, :, :]).then_inc(max_hi, 1)
                dve.wait_ge(max_hi, n + 1)
                nc.vector.tensor_tensor(max_split[:, :, 1, :], negmax[:, :, :], max_split[:, :, 0, :],
                                        ALU.subtract).then_inc(max_lo, 1)

            def attn_scale(grp):
                if not (isinstance(grp, int) and grp == 0):
                    dve.wait_ge(attn_ready, grp)
                dve.wait_ge(av_done, grp + 1)
                nc.vector.reciprocal(attn[:, :], den_ps[:, :]).then_inc(recip_done, 1)
                dve.wait_ge(recip_done, grp + 1)
                nc.vector.tensor_tensor(attn[:, :], out_ps[:, :], attn[:, :], ALU.mult).then_inc(attn_scaled, 1)

            def attn_lo(grp, g):
                dve.wait_ge(attn_rounded, grp + 1)
                nc.vector.scalar_tensor_tensor(attnT[:, 1, g, :], attn[:, :], bvc[:, g:g + 1],
                                               attnT[:, 0, g, :].bitcast(FP32), ALU.add, ALU.subtract).then_inc(attn_ready, 1)

            def ff_lo(i):
                to, _, raw = ff_weights[i]
                dve.wait_ge(ff_rounded, i + 1)
                nc.vector.tensor_tensor(to[:, 1], raw, to[:, 0].bitcast(FP32), ALU.subtract).then_inc(ff_split, 1)

            def out_tile(b, at, kind, t):
                key = ("tail" if kind == "tail" else "o", t)
                dve.wait_ge(gen_ready, use(at, kind, key) + 1)
                dve.wait_ge(residual_ready, b * NT + t + 1)
                nc.vector.tensor_tensor(xbuf[:, t, :], bank(kind, key)[:, :], xbuf[:, t, :], ALU.add).then_inc(emptied[bank_of(kind, key)], 1)

            for t in range(NT):
                token_lo(None, "ahead", "c", t)
            dve.wait_ge(x_loaded, 16)
            for t in range(NT):
                tile_stats(t)
            mean_and_variance(0)
            weight_lo(0)
            normalise(0, range(NT))
            dve.wait_ge(small_loaded, 48)
            lo(qk[:, KLO, :], qk[:, KHI, :], None, "ahead", ("k", -2), bkc[:, 0:1])
            for t in range(NT):
                token_lo(None, "ahead", "x", t)
            weight_lo(1)
            lo(qk[:, QLO, :], qk[:, QHI, :], None, "ahead", ("q", -2), bqc[:, 0:1])
            weight_lo(2)
            weight_lo(3)
            dve.wait_ge(gen_ready, use(None, "ahead", ("bo",)) + 1)
            nc.vector.tensor_copy(bo_all[:, :], bank("ahead", ("bo",))[:, :]).then_inc(emptied[bank_of("ahead", ("bo",))], 1)
            lo(qk[:, KLO, :], qk[:, KHI, :], None, "ahead", ("k", -1), bkc[:, 1:2])
            lo(qk[:, QLO, :], qk[:, QHI, :], None, "ahead", ("q", -1), bqc[:, 1:2])
            for u in range(UNITS):
                maxima(0, u)
            split_maxima(0)

            def step(b, kind, odd=None):
                for g in range(NG):
                    grp = b * NG + g
                    mt = (g + 2) % NG

                    def q_lo():
                        lo(qk[:, QLO, :], qk[:, QHI, :], b, kind, ("q", g), bqc[:, mt:mt + 1])

                    def k_lo():
                        lo(qk[:, KLO, :], qk[:, KHI, :], b, kind, ("k", g), bkc[:, mt:mt + 1])

                    if g == 1 and kind != "first":
                        out_tile(b - 1, b, kind, 2)
                        out_tile(b - 1, b, kind, 3)
                    if g == 2 and kind != "last":
                        normalise(b + 1, range(NT))
                        token_lo(b, kind, "c", 3)
                        token_lo(b, kind, "x", 0)
                        token_lo(b, kind, "x", 1)
                    if not looks_ahead(kind, g):
                        attn_lo(grp - 1, (g - 1) % NG)
                    if looks_ahead(kind, g):
                        for u in range(UNITS):
                            maxima(b * GROUP + (g + 1) * UNITS, u)
                            if g == 2 and kind != "last" and u in X_LATE:
                                token_lo(b, kind, "x", X_LATE[u])
                            if projects(kind, g) and g != 2 and u == 1:
                                q_lo()
                            if not (kind == "first" and g == 0) and u == 2:
                                attn_lo(grp - 1, (g - 1) % NG)
                            if projects(kind, g) and u == k_at(kind, g) and g != 1:
                                k_lo()
                            if g == 0 and kind != "first" and u == 8:
                                out_tile(b - 1, b, kind, 0)
                            if g == 2 and kind != "last" and u == 8:
                                q_lo()
                        split_maxima(grp + 1)
                        if projects(kind, g) and g == 1:
                            k_lo()
                    if g == 1 and kind != "last":
                        token_lo(b, kind, "c", 0)
                        token_lo(b, kind, "c", 1)
                        dve.wait_ge(x_loaded, b * 32 + 32)
                        for t in range(NT):
                            tile_stats(t)
                        mean_and_variance(b + 1)
                        token_lo(b, kind, "c", 2)
                    if g == 3 and kind == "last":
                        dve.wait_ge(xa_loaded, 16 * NT)
                        for t in range(NT):
                            nc.vector.bn_stats(stats[:, t, :], kept.xa[:, t, :]).then_inc(stats_done, 1)
                        mean_and_variance(B)
                        continue
                    attn_scale(grp)
                    if g == 0 and kind != "first":
                        out_tile(b - 1, b, kind, 1)

            steps(dve, step)
            done = B * NG - 1
            dve.wait_ge(attn_ready, done)
            dve.wait_ge(av_done, done + 1)
            for t in range(NT + 1):
                if t < NT:
                    cols = slice(t * P, (t + 1) * P)
                    nc.vector.reciprocal(attn[:, cols], den_ps[:, cols]).then_inc(recip_done, 1)
                    dve.wait_ge(recip_done, done + t + 1)
                    nc.vector.tensor_tensor(attn[:, cols], out_ps[:, cols], attn[:, cols], ALU.mult).then_inc(attn_scaled, 1)
                if t >= 1:
                    cols = slice((t - 1) * P, t * P)
                    dve.wait_ge(attn_rounded, done + t)
                    nc.vector.scalar_tensor_tensor(attnT[:, 1, NG - 1, cols], attn[:, cols], bvc[:, NG - 1:NG],
                                                   attnT[:, 0, NG - 1, cols].bitcast(FP32), ALU.add, ALU.subtract).then_inc(attn_ready, 1)
            dve.wait_ge(rstd_done, B + 1)
            for t in range(NT):
                nc.vector.tensor_scalar(kept.xn[:, t, :], kept.xa[:, t, :], mv[:, t, 0:1], rstd[:, t:t + 1],
                                        ALU.subtract, ALU.mult).then_inc(normed, 1)
            for t in range(NT):
                out_tile(B - 1, None, "tail", t)
                if t < NT - 1:
                    ff_lo(t + 1)

        @block.tensor
        def _(pe):
            def claim(b, kind, key):
                if kind != "ahead" or use(b, kind, key) >= 2:
                    pe.wait_ge(emptied[bank_of(kind, key)], bank_use(b, kind, key))
                return bank(kind, key)

            def transposed(ps, of):
                for k in range(4):
                    done = nc.tensor.transpose(ps[:, k * P:(k + 1) * P], of(k), ident[:, :])
                return done

            def product(b, kind, key):
                ps = claim(b, kind, key)
                name, n = key
                if key == ("q", 2):
                    pe.wait_ge(*has_left(b, kind, ("x", NT - 2)))
                    pe.wait_ge(*has_left(b, kind, ("x", NT - 1)))
                if name == "tail":
                    pe.wait_ge(attn_ready, B * NG + n)
                if key == ("o", 0):
                    pe.wait_ge(attn_ready, b * NG)
                cols = slice(((n + 2) if name in "qk" else n) % NK * P, ((n + 2) if name in "qk" else n) % NK * P + P)
                for k in range(NK):
                    for i, j in TERMS:
                        stationary, moving = {"q": (wqT[:, i, k, cols], xnT[:, j, k, :]), "k": (wkT[:, i, k, cols], cxT[:, j, k, :]),
                                       "v": (cxT[:, i, k, cols], wvT[:, j, k, :]), "o": (attnT[:, i, k, cols], woT[:, j, k, :])}["o" if name == "tail" else name]
                        done = nc.tensor.matmul(ps[:, :], stationary, moving, start=(k == 0 and (i, j) == TERMS[0]),
                                                stop=(k == NK - 1 and (i, j) == TERMS[-1]))
                        if k == NK - 1 and (i, j) == TERMS[-1]:
                            done.then_inc(gen_ready, 1)
                        yield

            def products(b, kind, which):
                for key in which:
                    yield from product(b, kind, key)

            def whole(made):
                for _ in made:
                    pass

            def weight(i):
                pe.wait_ge(w_loaded[i], 16)
                for k in range(NK):
                    n = i * NK + k
                    if n >= 6:
                        pe.wait_ge(w_split, n - 5)
                    transposed(weight_ps[n % 6], lambda m: WEIGHTS[i][1][:, m, k * P:(k + 1) * P]).then_inc(w_ready, 1)

            def c_tile(b, kind, t, half):
                ps = claim(b, kind, ("c", t))
                transposed(ps, lambda k: vc[:, half, t, k * P:(k + 1) * P]).then_inc(gen_ready, 1)

            def x_tile(b, kind, t):
                ps = claim(b, kind, ("x", t))
                pe.wait_ge(normed, (0 if kind == "ahead" else b + 1) * NT + (t + 1))
                transposed(ps, lambda k: xbuf[:, t, k * P:(k + 1) * P]).then_inc(gen_ready, 1)

            def max_unit(units, slot, u):
                if not (isinstance(units, int) and units + u < 2):
                    pe.wait_ge(max_done, units + u - 1)
                kind, j = unit(u)
                ps = max_ps[u % 2]

                def scores(h, qt, c0, c1):
                    nc.tensor.matmul(ps[:, c0:c1], qs[0:M_ROW, slot, 0, h, qt * P:(qt + 1) * P],
                                     qs[0:M_ROW, slot, 1, h, 0:c1 - c0], start=True, stop=False)

                def mask(c):
                    return nc.tensor.matmul(ps[:, c:c + P], ident16[:, :], mask16[:, :], start=False, stop=True)

                if kind == "A":
                    scores(j, 3, 0, S)
                    done = mask(3 * P)
                elif kind == "B":
                    scores(j, 0, 0, 2 * P)
                    mask(0)
                    scores(j, 2, P, S)
                    done = mask(3 * P)
                else:
                    for i in range(2):
                        scores(2 * j + i, 1, i * 2 * P, (i + 1) * 2 * P)
                        done = mask((2 * i + 1) * P)
                done.then_inc(max_ready, 1)

            def score_unit(units, slot, u):
                if not (isinstance(units, int) and units + u < 2):
                    pe.wait_ge(exp_done, units + u - 1)
                kind, j = unit(u)
                ps = score_ps[u % 2]

                def scores(h, kt, q0, c0, c1):
                    return nc.tensor.matmul(ps[:, c0:c1], qs[:, slot, 1, h, kt * P:(kt + 1) * P],
                                            qs[:, slot, 0, h, q0:q0 + c1 - c0], start=True, stop=True)

                if kind == "A":
                    done = scores(j, 0, 0, 0, S)
                elif kind == "B":
                    scores(j, 3, 2 * P, 2 * P, S)
                    done = scores(j, 1, P, 0, 3 * P)
                else:
                    scores(2 * j, 2, 2 * P, 0, 2 * P)
                    done = scores(2 * j + 1, 2, 2 * P, 2 * P, S)
                done.then_inc(score_ready, 1)

            def maxima_across(b, kind, g, n):
                ps = claim(b, kind, ("m", g))
                pe.wait_ge(max_lo, n + 1)
                for t in range(NT):
                    done = nc.tensor.transpose(ps[0:2 * HG, t * P:(t + 1) * P],
                                               max_split[:, t, :, :].rearrange("p s h -> p (s h)"), ident[:, :])
                done.then_inc(gen_ready, 1)

            def weigh(g, kt, half, of):
                for h in range(HG):
                    done = nc.tensor.matmul(out_ps[h * HD:(h + 1) * HD, kt * P:S],
                                            vc[:, half, kt, g * P + h * HD:g * P + (h + 1) * HD], of(h),
                                            start=(kt == 0), stop=(kt == 2))
                return done

            pe.wait_ge(ident_made, 1)
            pe.wait_ge(ctx_loaded, 16)
            for t in range(NT):
                c_tile(None, "ahead", t, 0)
            weight(0)
            weight(1)
            pe.wait_ge(w_split, NK)
            pe.wait_ge(*has_left(None, "ahead", ("c", NT - 2)))
            pe.wait_ge(*has_left(None, "ahead", ("c", NT - 1)))
            whole(product(None, "ahead", ("k", -2)))
            for t in range(NT):
                x_tile(None, "ahead", t)
            pe.wait_ge(w_split, 2 * NK)
            pe.wait_ge(*has_left(None, "ahead", ("x", NT - 2)))
            pe.wait_ge(*has_left(None, "ahead", ("x", NT - 1)))
            whole(product(None, "ahead", ("q", -2)))
            weight(2)
            weight(3)
            pe.wait_ge(bo_loaded, 16)
            pe.wait_ge(const_step, 7)
            nc.tensor.matmul(claim(None, "ahead", ("bo",))[:, :], ones_row[:, :], attn[0:1, :],
                             start=True, stop=True).then_inc(gen_ready, 1)
            pe.wait_ge(w_split, 3 * NK)
            whole(products(None, "ahead", [("v", 0), ("v", 1)]))
            whole(products(None, "ahead", [("k", -1), ("q", -1)]))
            pe.wait_ge(w_split, 4 * NK)
            pe.wait_ge(stacked, 16 * STACK_DMAS)
            for u in range(UNITS):
                max_unit(0, 0, u)
            maxima_across(None, "ahead", -1, 0)
            whole(products(None, "ahead", [("v", 2), ("v", 3)]))

            pa, pb, pc = probs[:, 0:HG, :], probs[:, HG:2 * HG, :], probs[:, 2 * HG:UNITS, :]

            def step(b, kind, odd=None):
                half = b % 2 if odd is None else odd
                for g in range(NG):
                    grp = b * NG + g
                    units = b * GROUP + g * UNITS

                    def filling(which):
                        fill = products(b, kind, which)
                        rest = [len(which) * NK * len(TERMS)]

                        def go(n):
                            for _ in range(min(n, rest[0])):
                                next(fill)
                                rest[0] -= 1
                            if not rest[0]:
                                next(fill, None)
                        return rest, go

                    prepares = g == 2 and kind != "last"
                    if prepares:
                        whole(product(b, kind, ("v", 0)))
                        c_tile(b, kind, 2, 1 - half)
                    rest, go = filling([("v", 1)] if prepares else with_scores(kind, g))
                    if not prepares:
                        go(LEAD[g])
                    pe.wait_ge(m_stacked, grp * 32 + 32)
                    for u in range(UNITS):
                        score_unit(units, g % 2, u)
                        go(-(-rest[0] // max(1, (V1_BY if prepares else UNITS) - u)))
                        if prepares and u == V1_BY:
                            c_tile(b, kind, 3, 1 - half)
                        if prepares and u in X_AT:
                            x_tile(b, kind, X_AT.index(u))

                    rest, go = filling(with_maxima(kind, g))
                    if looks_ahead(kind, g):
                        pe.wait_ge(stacked, (grp + 2) * (16 * STACK_DMAS))
                    for u in range(UNITS):
                        if looks_ahead(kind, g):
                            max_unit(units + UNITS, (g + 1) % 2, u)
                        if prepares and u in X_LATE:
                            x_tile(b, kind, X_LATE[u])
                        if prepares and u == 0:
                            pe.wait_ge(*has_left(b, kind, ("c", 3)))
                        if u == AV0_AT:
                            pe.wait_ge(masked, grp * 4 + 1)
                            if g == 0:
                                prior = {"first": "ahead", "mid": "first", "last": "mid"}[kind]
                                pe.wait_ge(emptied[bank_of(prior, ("v", NT - 1))], before(b, kind, lambda l: len(l) // 2))
                            if not (g == 0 and kind == "first"):
                                pe.wait_ge(attn_scaled, grp)
                            weigh(g, 0, half, lambda h: pa[:, h, :]).then_inc(av0_done, 1)
                        if u >= 2:
                            go(-(-rest[0] // max(1, products_by(kind, g) - u)))
                        if u == AV1_AT:
                            pe.wait_ge(masked, grp * 4 + 3)
                            weigh(g, 1, half, lambda h: pb[:, h, 0:S - K_LO])

                    go(rest[0])

                    weigh(g, 3, half, lambda h: pb[:, h, K_HI:S])
                    pe.wait_ge(masked, grp * 4 + 4)
                    weigh(g, 2, half, lambda h: pc[:, h // 2, (h % 2) * K_MID:(h % 2 + 1) * K_MID])
                    if looks_ahead(kind, g):
                        maxima_across(b, kind, g, grp + 1)
                    if g == 1 and kind != "last":
                        pe.wait_ge(ctx_loaded, b * 16 + 32)
                        c_tile(b, kind, 0, 1 - half)
                    if kind == "last" and g == NG - 1:
                        for kt, of in ((0, lambda h: pa[:, h, :]), (1, lambda h: pb[:, h, 0:S - K_LO]), (3, lambda h: pb[:, h, K_HI:S]),
                                       (2, lambda h: pc[:, h // 2, (h % 2) * K_MID:(h % 2 + 1) * K_MID])):
                            for h in range(HG):
                                done = nc.tensor.matmul(den_ps[h * HD:(h + 1) * HD, kt * P:S], ones32[:, :], of(h),
                                                        start=(kt == 0), stop=(kt == 2))
                    else:
                        pe.wait_ge(folded, grp * 3 + 3)
                        for h in range(HG):
                            done = nc.tensor.matmul(den_ps[h * HD:(h + 1) * HD, :], ones32[:, :], pa[:, h, :], start=True, stop=True)
                    done.then_inc(av_done, 1)

                    if g == 0 and kind != "first":
                        whole(product(b, kind, ("o", 1)))
                    if g == 1 and kind != "last":
                        c_tile(b, kind, 1, 1 - half)
                    if g == 3 and kind != "last":
                        whole(product(b, kind, ("v", 3)))

            steps(pe, step)
            whole(products(None, "tail", [("tail", t) for t in range(NT)]))


def ffn_phase(nc, kept, x1_dram, out):
    with ExitStack() as ctx:
        def sb(name, shape, dt=FP32):
            return ctx.enter_context(nc.sbuf_tensor(name, shape, dt))

        def sem(name):
            return ctx.enter_context(nc.semaphore(name))

        RING = 8
        BANKS = 4
        LAG = 4
        GENS = 3

        u1, v1, u2, v2, b1c, b2_row = kept.u1, kept.v1, kept.u2, kept.v2, kept.b1c, kept.b2_row
        ident, ones_row, minus_half, xa, xn = kept.ident, kept.ones_row, kept.minus_half, kept.xa, kept.xn
        b2_all = sb("b2_all", [P, D])
        y = sb("y", [P, NT, D])
        result = sb("result", [P, NT, D])
        xnT = sb("xn2T", [P, 2, NK, S], F32R)
        pT = sb("pT", [P, 2, S], F32R)
        qT = sb("qT", [P, 2, S], F32R)
        gelu = sb("gelu", [P, RING, S])
        hT = sb("hT", [P, RING, 2, S], F32R)
        stats = sb("stats2", [P, NT, 6])
        mv = sb("mv2", [P, NT, 2])
        rstd = sb("rstd2", [P, NT])
        varp = sb("varp2", [P, NT])

        psum = [ctx.enter_context(nc.psum_tensor(f"psf{i}", [P, 512], FP32)) for i in range(8)]
        h_ps, gen_ps, q_ps = psum[0:BANKS], psum[BANKS:BANKS + GENS], psum[7]

        x_loaded = sem("f_x_loaded")
        gen_ready = sem("f_gen_ready")
        rounded = sem("f_rounded")
        evacuated = sem("f_evacuated")
        h_ready = sem("h_ready")
        gelu_done = sem("gelu_done")
        h_rounded = sem("h_rounded")
        h_split = sem("h_split")
        h_used = sem("h_used")
        q_rounded = sem("q_rounded")
        q_split = sem("q_split")
        stats_done = sem("f_stats_done")
        mv_done = sem("f_mv_done")
        var_done = sem("f_var_done")
        rstd_done = sem("f_rstd_done")
        normed = sem("f_normed")
        y_ready = sem("y_ready")
        stored = sem("stored")

        FIRST = ["b2"] + [("x", t) for t in range(NT)] + ["p"]
        STEP = [("x", t) for t in range(NT)] + ["p"] + [("o", t) for t in range(NT)]
        assert len(FIRST) % GENS == 0 and len(STEP) % GENS == 0
        LAST = [("o", t) for t in range(NT)]

        def use(j, last, key):
            if j is None:
                return FIRST.index(key)
            return j * len(STEP) + (len(FIRST) + (LAST if last else STEP).index(key))

        def bank(j, last, key):
            l = FIRST if j is None else LAST if last else STEP
            return gen_ps[l.index(key) % GENS]

        def splits(j, t):
            return t if j is None else j * (NT + 1) + (NT + 1 + t)

        T_AT = {12: 0, 13: 1, 14: 2, 15: 3}

        block = ctx.enter_context(nc.Block())

        @block.sync
        def _(sp):
            def load(j, t):
                sp.dma_start(xa[:, t, :], x1_dram[bass.ds(j, 1), t * P:(t + 1) * P, :].rearrange("a p d -> (a p) d")).then_inc(x_loaded, 16)

            def step(j, last):
                if not last:
                    for t in range(NT):
                        sp.wait_ge(y_ready, j * NT + t + 1)
                        load(j + 1, t)
                for t in range(NT):
                    sp.wait_ge(evacuated, use(j, last, ("o", t)) + 1)
                    sp.dma_start(out[bass.ds(j, 1), t * P:(t + 1) * P, :].rearrange("a p d -> (a p) d"),
                                 result[:, t, :]).then_inc(stored, 16)

            with sp.Fori(0, B - 1) as j:
                step(j, False)
            step(B - 1, True)
            sp.wait_ge(stored, 16 * NT * B)

        @block.gpsimd
        def _(pool):
            def rstds(done):
                wait_apart(pool, y_ready, NT, mv_done, done * NT + NT)
                pool.tensor_scalar(varp[:, :], mv[:, :, 1], EPS, None, ALU.add).then_inc(var_done, 1)
                pool.wait_ge(var_done, done + 1)
                pool.tensor_tensor(rstd[:, :], varp[:, :], minus_half[:, :], ALU.pow).then_inc(rstd_done, 1)

            def step(j, last):
                if isinstance(j, int) and j == 0:
                    pool.wait_ge(evacuated, 1)
                else:
                    pool.wait_ge(x_loaded, j * (16 * NT))
                    pool.wait_ge(normed, j * NT)
                    pool.wait_ge(evacuated, use(j, False, STEP[0]))
                for t in range(NT):
                    pool.tensor_tensor(y[:, t, :], xa[:, t, :], b2_all[:, :], ALU.add).then_inc(y_ready, 1)
                if not last:
                    rstds(j)

            step(0, False)
            with pool.Fori(1, B - 1) as j:
                step(j, False)
            step(B - 1, True)

        @block.scalar
        def _(act):
            def tile_hi(j, t):
                act.wait_ge(gen_ready, use(j, False, ("x", t)) + 1)
                nc.scalar.activation(xnT[:, 0, :, t * P:(t + 1) * P],
                                     bank(j, False, ("x", t))[:, :].rearrange("p (k t) -> p k t", k=NK), ACT.Copy).then_inc(rounded, 1)

            def p_hi(j):
                act.wait_ge(gen_ready, use(j, False, "p") + 1)
                nc.scalar.activation(pT[:, 0, :], bank(j, False, "p")[:, :], ACT.Copy).then_inc(rounded, 1)

            for t in range(NT):
                tile_hi(None, t)
            p_hi(None)

            def step(j, last):
                tiles = j * NF
                for m in range(NF + 1):
                    if m < NF:
                        act.wait_ge(h_ready, tiles + m + 1)
                        if not (isinstance(j, int) and j == 0 and m < RING):
                            act.wait_ge(h_split, tiles + m + 1 - RING)
                        nc.scalar.activation(gelu[:, m % RING, :], h_ps[m % BANKS][:, :], ACT.Gelu_apprx_tanh,
                                             bias=b1c[:, m:m + 1]).then_inc(gelu_done, 1)
                    if m >= 1:
                        n = m - 1
                        act.wait_ge(gelu_done, tiles + n + 1)
                        if not (isinstance(j, int) and j == 0 and n < RING):
                            act.wait_ge(h_used, tiles + n + 1 - RING)
                        nc.scalar.activation(hT[:, n % RING, 0, :], gelu[:, n % RING, :], ACT.Copy).then_inc(h_rounded, 1)
                    if not last and m - 1 in T_AT:
                        tile_hi(j, T_AT[m - 1])
                act.wait_ge(h_used, tiles + NF)
                nc.scalar.activation(qT[:, 0, :], q_ps[:, :], ACT.Copy).then_inc(q_rounded, 1)
                if not last:
                    p_hi(j)

            step(0, False)
            with act.Fori(1, B - 1) as j:
                step(j, False)
            step(B - 1, True)

        @block.vector
        def _(dve):
            def minus(out, whole, hi_half):
                return nc.vector.tensor_tensor(out, whole, hi_half.bitcast(FP32), ALU.subtract)

            def tile_lo(j, t):
                dve.wait_ge(rounded, splits(j, t) + 1)
                cols = slice(t * P, (t + 1) * P)
                minus(xnT[:, 1, :, cols], bank(j, False, ("x", t))[:, :].rearrange("p (k t) -> p k t", k=NK),
                      xnT[:, 0, :, cols]).then_inc(evacuated, 1)

            def p_lo(j):
                dve.wait_ge(rounded, splits(j, NT) + 1)
                minus(pT[:, 1, :], bank(j, False, "p")[:, :], pT[:, 0, :]).then_inc(evacuated, 1)

            def norm_stats(done, t):
                dve.wait_ge(x_loaded, done * (16 * NT) + 16 * NT)
                nc.vector.bn_stats(stats[:, t, :], xa[:, t, :]).then_inc(stats_done, 1)

            def mean_and_variance(done):
                for t in range(NT):
                    wait_apart(dve, evacuated, 1, stats_done, done * NT + t + 1)
                    nc.vector.bn_aggr(mv[:, t, :], stats[:, t, :]).then_inc(mv_done, 1)

            def normalise(done, t):
                dve.wait_ge(rstd_done, done + 1)
                nc.vector.tensor_scalar(xn[:, t, :], xa[:, t, :], mv[:, t, 0:1], rstd[:, t:t + 1],
                                        ALU.subtract, ALU.mult).then_inc(normed, 1)

            dve.wait_ge(gen_ready, 1)
            nc.vector.tensor_copy(b2_all[:, :], bank(None, False, "b2")[:, :]).then_inc(evacuated, 1)
            for t in range(NT):
                tile_lo(None, t)
            p_lo(None)

            def step(j, last):
                tiles = j * NF
                for m in range(NF):
                    dve.wait_ge(h_rounded, tiles + m + 1)
                    minus(hT[:, m % RING, 1, :], gelu[:, m % RING, :], hT[:, m % RING, 0, :]).then_inc(h_split, 1)
                    if not last:
                        if 4 <= m < 4 + NT:
                            norm_stats(j, m - 4)
                        if m == 4 + NT - 1:
                            mean_and_variance(j)
                        if 8 < m <= 8 + NT:
                            normalise(j, m - 9)
                        if m in T_AT:
                            tile_lo(j, T_AT[m])
                dve.wait_ge(q_rounded, j + 1)
                minus(qT[:, 1, :], q_ps[:, :], qT[:, 0, :]).then_inc(q_split, 1)
                if not last:
                    p_lo(j)
                if not (isinstance(j, int) and j == 0):
                    dve.wait_ge(stored, j * (16 * NT))
                for t in range(NT):
                    dve.wait_ge(gen_ready, use(j, last, ("o", t)) + 1)
                    dve.wait_ge(y_ready, j * NT + t + 1)
                    nc.vector.tensor_tensor(result[:, t, :], bank(j, last, ("o", t))[:, :], y[:, t, :], ALU.add).then_inc(evacuated, 1)

            step(0, False)
            with dve.Fori(1, B - 1) as j:
                step(j, False)
            step(B - 1, True)

        @block.tensor
        def _(pe):
            def claim(j, last, key):
                n = use(j, last, key)
                if j is not None or n >= GENS:
                    pe.wait_ge(evacuated, n - GENS + 1)
                return bank(j, last, key)

            def summed(ps, terms):
                for n, (left, right) in enumerate(terms):
                    done = nc.tensor.matmul(ps[:, :], left, right, start=(n == 0), stop=(n == len(terms) - 1))
                return done

            def tile(j, t):
                ps = claim(j, False, ("x", t))
                if j is not None:
                    pe.wait_ge(normed, j * NT + (t + 1))
                for k in range(NK):
                    done = nc.tensor.transpose(ps[:, k * P:(k + 1) * P], xn[:, t, k * P:(k + 1) * P], ident[:, :])
                done.then_inc(gen_ready, 1)

            def first_product(j):
                ps = claim(j, False, "p")
                pe.wait_ge(evacuated, use(j, False, ("x", NT - 1)) + 1)
                summed(ps, [(u1[:, i, k, :], xnT[:, i2, k, :]) for k in range(NK) for i, i2 in TERMS]).then_inc(gen_ready, 1)

            nc.tensor.matmul(bank(None, False, "b2")[:, :], ones_row[:, :], b2_row[:, :], start=True, stop=True).then_inc(gen_ready, 1)
            for t in range(NT):
                tile(None, t)
            first_product(None)

            def step(j, last):
                tiles = j * NF
                pe.wait_ge(evacuated, (use(None, False, "p") if isinstance(j, int) and j == 0 else use(j - 1, False, "p")) + 1)
                for m in range(NF + LAG):
                    if m < NF:
                        if not (isinstance(j, int) and j == 0 and m < BANKS):
                            pe.wait_ge(gelu_done, tiles + m + 1 - BANKS)
                        summed(h_ps[m % BANKS], [(v1[:, i, m * P:(m + 1) * P], pT[:, i2, :]) for i, i2 in TERMS]).then_inc(h_ready, 1)
                    if m >= LAG:
                        n = m - LAG
                        if n == 0 and not (isinstance(j, int) and j == 0):
                            pe.wait_ge(q_split, j)
                        pe.wait_ge(h_split, tiles + n + 1)
                        for i, (w, a) in enumerate(TERMS):
                            done = nc.tensor.matmul(q_ps[:, :], u2[:, w, n, :], hT[:, n % RING, a, :],
                                                    start=(n == 0 and i == 0), stop=(n == NF - 1 and i == 2))
                        done.then_inc(h_used, 1)
                    if not last and m in T_AT:
                        tile(j, T_AT[m])
                if not last:
                    first_product(j)
                pe.wait_ge(q_split, j + 1)
                for t in range(NT):
                    ps = claim(j, last, ("o", t))
                    summed(ps, [(qT[:, i, t * P:(t + 1) * P], v2[:, i2, :]) for i, i2 in TERMS]).then_inc(gen_ready, 1)

            step(0, False)
            with pe.Fori(1, B - 1) as j:
                step(j, False)
            step(B - 1, True)


_INS = ["x", "ctx_1024", "L0_xattn_Wq", "L0_xattn_bq", "L0_xattn_Wk", "L0_xattn_bk", "L0_xattn_Wv", "L0_xattn_bv",
        "L0_xattn_Wo", "L0_xattn_bo", "L0_ffn_U1", "L0_ffn_V1", "L0_ffn_b1", "L0_ffn_U2", "L0_ffn_V2", "L0_ffn_b2"]


def build(nc, a, out):
    x1_dram = nc.dram_tensor("x1_scratch", (B, S, D), FP32).ap()
    with ExitStack() as ctx:
        kept = Kept(nc, ctx)
        attention_phase(nc, kept, a["x"], a["ctx_1024"], *(a[f"L0_xattn_{n}"] for n in ("Wq", "bq", "Wk", "bk", "Wv", "bv", "Wo", "bo")),
                        x1_dram, *(a[f"L0_ffn_{n}"] for n in ("U1", "V1", "b1", "U2", "V2", "b2")))
        ffn_phase(nc, kept, x1_dram, out)


def kernel(**inputs):
    import numpy as _np
    import concourse.bacc as _bacc
    from concourse.bass_utils import run_bass_kernel_spmd as _run

    nc = _bacc.Bacc("TRN2", target_bir_lowering=False, num_devices=1)
    arrays, args = {}, {}
    for name in _INS:
        a = _np.ascontiguousarray(inputs[name])
        arrays[f"in_{name}_dram"] = a
        args[name] = nc.dram_tensor(f"in_{name}_dram", a.shape, mybir.dt.from_np(a.dtype), kind="ExternalInput").ap()
    out = nc.dram_tensor("out_0_dram", (B, S, D), FP32, kind="ExternalOutput").ap()
    build(nc, args, out)
    r = _run(nc, [arrays], core_ids=[0])
    return r.results[0]["out_0_dram"]
```
